# Optimizing a Trainium2 kernel written in Bass

```python
import numpy as np
import jax
import jax.numpy as jnp

def _softmax(x, axis=-1):
    return jax.nn.softmax(x, axis=axis)

def _gelu(x):
    return jax.nn.gelu(x, approximate=True)

def _silu(x):
    return jax.nn.silu(x)

def _sigmoid(x):
    return jax.nn.sigmoid(x)

def _layernorm(x, axis=-1, eps=1e-05):
    m = jnp.mean(x, axis=axis, keepdims=True)
    v = jnp.var(x, axis=axis, keepdims=True)
    return (x - m) / jnp.sqrt(v + eps)

def _scatter_add(tgt, idx, src, axis=0):
    return tgt.at[idx].add(src)

def _segment_sum(src, seg, n):
    return jax.ops.segment_sum(src, seg, n)
kernel_name = 'mk_seq_preln_d2_jaxref_r8_cfae67'

def setup_inputs(seed: int=0):
    np.random.seed(seed)
    _w = jnp.asarray

    def _L0_attn_setup():
        import jax, jax.numpy as jnp
        import numpy as np
        EMBED_DIM = 128
        NUM_HEADS = 8
        HEAD_DIM = EMBED_DIM // NUM_HEADS
        NUM_QUBITS = 8
        CIRCUITS = 4
        DEPTH = 3
        WAVELENGTHS = 16
        SCALING = HEAD_DIM ** (-0.5)
        ERR_MIN = 1e-06
        TWO_PI = 2.0 * np.pi

        def _quantum_encode(x, photonic_phases):
            hd = x.shape[-1]
            norm = jnp.sqrt(jnp.sum(x * x, axis=-1, keepdims=True))
            normed = x / jnp.maximum(norm, 1e-12)
            ch = jnp.arange(hd)
            phases = photonic_phases[ch % WAVELENGTHS, ch]
            return normed * jnp.exp(1j * phases)

        def _entangle(state, gates):
            for depth in range(DEPTH):
                g = gates[depth, :NUM_HEADS - 1]
                theta = g[:, 0][None, None, :, None]
                phi = g[:, 1][None, None, :, None]
                s1 = state[:, :, :-1]
                s2 = state[:, :, 1:]
                cos_t = jnp.cos(theta / 2)
                sin_t = jnp.sin(theta / 2)
                ctrl = jnp.abs(s1) ** 2
                rot = cos_t * s2 + sin_t * jnp.exp(1j * phi) * jnp.conj(s2)
                new = ctrl * rot + (1.0 - ctrl) * s2
                state = jnp.concatenate([new, state[:, :, -1:]], axis=2)
            return state

        def _forward(query, W_qkv, b_qkv, W_out, b_out, quantum_weights, photonic_phases, entanglement_gates, superposition_logits):
            B, S, E = query.shape
            qkv = query @ W_qkv.T + b_qkv
            q, k, v = jnp.split(qkv, 3, axis=-1)
            q = q.reshape(B, S, NUM_HEADS, HEAD_DIM)
            k = k.reshape(B, S, NUM_HEADS, HEAD_DIM)
            v = v.reshape(B, S, NUM_HEADS, HEAD_DIM)
            qq = _quantum_encode(q, photonic_phases)
            kq = _quantum_encode(k, photonic_phases)
            vq = _quantum_encode(v, photonic_phases)
            q_ent = _entangle(qq, entanglement_gates)
            k_ent = _entangle(kq, entanglement_gates)
            coh = jnp.exp(1j * jnp.angle(jnp.sum(vq, axis=2, keepdims=True)))
            sup_w = jax.nn.softmax(superposition_logits)
            final = None
            for c in range(CIRCUITS):
                ratio = 0.5 + 0.3 * jnp.sin(quantum_weights[c, 0, 0])
                qa = jnp.sqrt(ratio) * q_ent
                ka = jnp.sqrt(1.0 - ratio) * k_ent
                pattern = jnp.einsum('bsid,bsjd->bsij', jnp.conj(qa), ka)
                mod = pattern * jnp.exp(1j * quantum_weights[c, 1, :])
                scores = jnp.abs(mod) ** 2 * SCALING
                probs = jax.nn.softmax(scores, axis=-1)
                amps = jnp.sqrt(probs + 1e-12)
                coh_phase = jnp.angle(jnp.sum(scores, axis=-1, keepdims=True))
                w = amps * jnp.cos(coh_phase)
                weighted = jnp.einsum('bsij,bsjd->bsid', w.astype(jnp.complex64), vq)
                co = weighted * coh
                amp = jnp.clip(jnp.abs(co), ERR_MIN, 1.0)
                ph = jnp.mod(jnp.angle(co), TWO_PI)
                corrected = amp * jnp.exp(1j * ph)
                contrib = sup_w[c] * corrected
                final = contrib if final is None else final + contrib
            measured = jnp.real(final).reshape(B, S, E)
            return measured @ W_out.T + b_out
        key = jax.random.key(seed)
        ks = jax.random.split(key, 8)
        B, S, E = (2, 256, EMBED_DIM)
        return {'query': jax.random.normal(ks[0], (B, S, E), jnp.float32), 'W_qkv': jax.random.normal(ks[1], (3 * E, E), jnp.float32) / np.sqrt(E).astype(np.float32), 'b_qkv': jnp.zeros((3 * E,), jnp.float32), 'W_out': jax.random.normal(ks[2], (E, E), jnp.float32) / np.sqrt(E).astype(np.float32), 'b_out': jnp.zeros((E,), jnp.float32), 'quantum_weights': jax.random.normal(ks[3], (CIRCUITS, NUM_QUBITS, NUM_QUBITS), jnp.float32) * 0.1, 'photonic_phases': jax.random.normal(ks[4], (WAVELENGTHS, E), jnp.float32) * np.float32(np.pi), 'entanglement_gates': jax.random.normal(ks[5], (DEPTH, NUM_HEADS, 4), jnp.float32) * 0.1, 'superposition_logits': jax.random.normal(ks[6], (CIRCUITS,), jnp.float32)}
    _L0_attn_in = _L0_attn_setup()

    def _L0_ffn_setup():
        import jax, jax.numpy as jnp
        import numpy as np
        DIM = 128
        HIDDEN = 384
        SCALE = 1.0 / 127.0

        def _dequant(w_int, dtype):
            return w_int.astype(dtype) * jnp.asarray(SCALE, dtype)
        key = jax.random.key(seed)
        k_x, k_g, k_u, k_d = jax.random.split(key, 4)
        x = jax.random.normal(k_x, (4, 256, DIM), dtype=jnp.float32)
        w_gate = jax.random.randint(k_g, (HIDDEN, DIM), -127, 128, dtype=jnp.int32)
        w_up = jax.random.randint(k_u, (HIDDEN, DIM), -127, 128, dtype=jnp.int32)
        w_down = jax.random.randint(k_d, (DIM, HIDDEN), -127, 128, dtype=jnp.int32)
        return {'x': x, 'w_gate': w_gate, 'w_up': w_up, 'w_down': w_down}
    _L0_ffn_in = _L0_ffn_setup()

    def _L1_attn_setup():
        import jax, jax.numpy as jnp
        import numpy as np
        B, S, D, H = (2, 256, 128, 16)
        DK = D // H
        SCALE = DK ** 0.5

        def _split_heads(t):
            b, s, d = t.shape
            return t.reshape(b, s, H, DK).transpose(0, 2, 1, 3)
        key = jax.random.key(seed)
        ks = jax.random.split(key, 5)
        std = 1.0 / np.sqrt(D)
        return {'x': jax.random.normal(ks[0], (B, S, D), dtype=jnp.float32), 'Wq': jax.random.normal(ks[1], (D, D), dtype=jnp.float32) * std, 'Wk': jax.random.normal(ks[2], (D, D), dtype=jnp.float32) * std, 'Wv': jax.random.normal(ks[3], (D, D), dtype=jnp.float32) * std, 'Wo': jax.random.normal(ks[4], (D, D), dtype=jnp.float32) * std}
    _L1_attn_in = _L1_attn_setup()

    def _L1_ffn_setup():
        import jax, jax.numpy as jnp
        import numpy as np
        B, S, H, E, K, F = (4, 256, 128, 8, 64, 512)
        key = jax.random.key(seed)
        k0, k1, k2, k3 = jax.random.split(key, 4)
        sc = lambda d: 1.0 / np.sqrt(d).astype(np.float32)
        return {'x': jax.random.normal(k0, (B, S, H), jnp.float32), 'Wg': jax.random.normal(k1, (E, H), jnp.float32) * sc(H), 'W1': jax.random.normal(k2, (E, H, F), jnp.float32) * sc(H), 'b1': jnp.zeros((E, F), jnp.float32), 'W2': jax.random.normal(k3, (E, F, H), jnp.float32) * sc(F), 'b2': jnp.zeros((E, H), jnp.float32)}
    _L1_ffn_in = _L1_ffn_setup()
    _d = {'L0_attn_query': _L0_attn_in['query'], 'L0_attn_W_qkv': _L0_attn_in['W_qkv'], 'L0_attn_b_qkv': _L0_attn_in['b_qkv'], 'L0_attn_W_out': _L0_attn_in['W_out'], 'L0_attn_b_out': _L0_attn_in['b_out'], 'L0_attn_quantum_weights': _L0_attn_in['quantum_weights'], 'L0_attn_photonic_phases': _L0_attn_in['photonic_phases'], 'L0_attn_entanglement_gates': _L0_attn_in['entanglement_gates'], 'L0_attn_superposition_logits': _L0_attn_in['superposition_logits'], 'L0_ffn_w_gate': _L0_ffn_in['w_gate'], 'L0_ffn_w_up': _L0_ffn_in['w_up'], 'L0_ffn_w_down': _L0_ffn_in['w_down'], 'L1_attn_Wq': _L1_attn_in['Wq'], 'L1_attn_Wk': _L1_attn_in['Wk'], 'L1_attn_Wv': _L1_attn_in['Wv'], 'L1_attn_Wo': _L1_attn_in['Wo'], 'L1_ffn_Wg': _L1_ffn_in['Wg'], 'L1_ffn_W1': _L1_ffn_in['W1'], 'L1_ffn_b1': _L1_ffn_in['b1'], 'L1_ffn_W2': _L1_ffn_in['W2'], 'L1_ffn_b2': _L1_ffn_in['b2']}
    _x0 = _d['L0_attn_query']
    _d['L0_attn_query'] = jax.random.normal(jax.random.fold_in(jax.random.key(seed), 1), (32, 256, 128), dtype=_x0.dtype)
    del _x0
    return _d

def reference(L0_attn_query, L0_attn_W_qkv, L0_attn_b_qkv, L0_attn_W_out, L0_attn_b_out, L0_attn_quantum_weights, L0_attn_photonic_phases, L0_attn_entanglement_gates, L0_attn_superposition_logits, L0_ffn_w_gate, L0_ffn_w_up, L0_ffn_w_down, L1_attn_Wq, L1_attn_Wk, L1_attn_Wv, L1_attn_Wo, L1_ffn_Wg, L1_ffn_W1, L1_ffn_b1, L1_ffn_W2, L1_ffn_b2):

    def _L0_attn_ref(query, W_qkv, b_qkv, W_out, b_out, quantum_weights, photonic_phases, entanglement_gates, superposition_logits):
        import jax, jax.numpy as jnp
        import numpy as np
        EMBED_DIM = 128
        NUM_HEADS = 8
        HEAD_DIM = EMBED_DIM // NUM_HEADS
        NUM_QUBITS = 8
        CIRCUITS = 4
        DEPTH = 3
        WAVELENGTHS = 16
        SCALING = HEAD_DIM ** (-0.5)
        ERR_MIN = 1e-06
        TWO_PI = 2.0 * np.pi

        def _quantum_encode(x, photonic_phases):
            hd = x.shape[-1]
            norm = jnp.sqrt(jnp.sum(x * x, axis=-1, keepdims=True))
            normed = x / jnp.maximum(norm, 1e-12)
            ch = jnp.arange(hd)
            phases = photonic_phases[ch % WAVELENGTHS, ch]
            return normed * jnp.exp(1j * phases)

        def _entangle(state, gates):
            for depth in range(DEPTH):
                g = gates[depth, :NUM_HEADS - 1]
                theta = g[:, 0][None, None, :, None]
                phi = g[:, 1][None, None, :, None]
                s1 = state[:, :, :-1]
                s2 = state[:, :, 1:]
                cos_t = jnp.cos(theta / 2)
                sin_t = jnp.sin(theta / 2)
                ctrl = jnp.abs(s1) ** 2
                rot = cos_t * s2 + sin_t * jnp.exp(1j * phi) * jnp.conj(s2)
                new = ctrl * rot + (1.0 - ctrl) * s2
                state = jnp.concatenate([new, state[:, :, -1:]], axis=2)
            return state

        def _forward(query, W_qkv, b_qkv, W_out, b_out, quantum_weights, photonic_phases, entanglement_gates, superposition_logits):
            B, S, E = query.shape
            qkv = query @ W_qkv.T + b_qkv
            q, k, v = jnp.split(qkv, 3, axis=-1)
            q = q.reshape(B, S, NUM_HEADS, HEAD_DIM)
            k = k.reshape(B, S, NUM_HEADS, HEAD_DIM)
            v = v.reshape(B, S, NUM_HEADS, HEAD_DIM)
            qq = _quantum_encode(q, photonic_phases)
            kq = _quantum_encode(k, photonic_phases)
            vq = _quantum_encode(v, photonic_phases)
            q_ent = _entangle(qq, entanglement_gates)
            k_ent = _entangle(kq, entanglement_gates)
            coh = jnp.exp(1j * jnp.angle(jnp.sum(vq, axis=2, keepdims=True)))
            sup_w = jax.nn.softmax(superposition_logits)
            final = None
            for c in range(CIRCUITS):
                ratio = 0.5 + 0.3 * jnp.sin(quantum_weights[c, 0, 0])
                qa = jnp.sqrt(ratio) * q_ent
                ka = jnp.sqrt(1.0 - ratio) * k_ent
                pattern = jnp.einsum('bsid,bsjd->bsij', jnp.conj(qa), ka)
                mod = pattern * jnp.exp(1j * quantum_weights[c, 1, :])
                scores = jnp.abs(mod) ** 2 * SCALING
                probs = jax.nn.softmax(scores, axis=-1)
                amps = jnp.sqrt(probs + 1e-12)
                coh_phase = jnp.angle(jnp.sum(scores, axis=-1, keepdims=True))
                w = amps * jnp.cos(coh_phase)
                weighted = jnp.einsum('bsij,bsjd->bsid', w.astype(jnp.complex64), vq)
                co = weighted * coh
                amp = jnp.clip(jnp.abs(co), ERR_MIN, 1.0)
                ph = jnp.mod(jnp.angle(co), TWO_PI)
                corrected = amp * jnp.exp(1j * ph)
                contrib = sup_w[c] * corrected
                final = contrib if final is None else final + contrib
            measured = jnp.real(final).reshape(B, S, E)
            return measured @ W_out.T + b_out
        return _forward(query, W_qkv, b_qkv, W_out, b_out, quantum_weights, photonic_phases, entanglement_gates, superposition_logits)

    def _L0_ffn_ref(x, w_gate, w_up, w_down):
        import jax, jax.numpy as jnp
        import numpy as np
        DIM = 128
        HIDDEN = 384
        SCALE = 1.0 / 127.0

        def _dequant(w_int, dtype):
            return w_int.astype(dtype) * jnp.asarray(SCALE, dtype)
        wg = _dequant(w_gate, x.dtype)
        wu = _dequant(w_up, x.dtype)
        wd = _dequant(w_down, x.dtype)
        gate = jnp.einsum('bsd,hd->bsh', x, wg)
        up = jnp.einsum('bsd,hd->bsh', x, wu)
        h = jax.nn.silu(gate) * up
        return jnp.einsum('bsh,dh->bsd', h, wd)

    def _L1_attn_ref(x, Wq, Wk, Wv, Wo):
        import jax, jax.numpy as jnp
        import numpy as np
        B, S, D, H = (2, 256, 128, 16)
        DK = D // H
        SCALE = DK ** 0.5

        def _split_heads(t):
            b, s, d = t.shape
            return t.reshape(b, s, H, DK).transpose(0, 2, 1, 3)
        b, s, d = x.shape
        q = _split_heads(x @ Wq)
        k = _split_heads(x @ Wk)
        v = _split_heads(x @ Wv)
        score = jnp.einsum('bhqd,bhkd->bhqk', q, k)
        causal = jnp.tril(jnp.ones((s, s), dtype=bool))[None, None]
        score = jnp.where(causal, score, -jnp.inf)
        attn = jax.nn.softmax(score / SCALE, axis=-1)
        out = jnp.einsum('bhqk,bhkd->bhqd', attn, v)
        out = out.transpose(0, 2, 1, 3).reshape(b, s, d)
        return out @ Wo

    def _L1_ffn_ref(x, Wg, W1, b1, W2, b2):
        import jax, jax.numpy as jnp
        import numpy as np
        B, S, H, E, K, F = (4, 256, 128, 8, 64, 512)
        b, s, h = x.shape
        logits = jnp.einsum('bsh,eh->bse', x, Wg)
        Sm = jnp.swapaxes(jax.nn.softmax(logits, axis=-1), 1, 2)
        G, I = jax.lax.top_k(Sm, K)
        ex = jnp.take_along_axis(x[:, None, :, :], I[..., None], axis=2)
        h1 = jax.nn.gelu(jnp.einsum('bekh,ehf->bekf', ex, W1) + b1[None, :, None, :])
        out = jnp.einsum('bekf,efh->bekh', h1, W2) + b2[None, :, None, :]
        out = G[..., None] * out
        new_x = jnp.zeros_like(x).at[jnp.arange(b)[:, None, None], I].add(out)
        return new_x
    x = L0_attn_query
    x = x + _L0_attn_ref(_layernorm(x, axis=-1), L0_attn_W_qkv, L0_attn_b_qkv, L0_attn_W_out, L0_attn_b_out, L0_attn_quantum_weights, L0_attn_photonic_phases, L0_attn_entanglement_gates, L0_attn_superposition_logits)
    x = x + _L0_ffn_ref(_layernorm(x, axis=-1), L0_ffn_w_gate, L0_ffn_w_up, L0_ffn_w_down)
    x = x + _L1_attn_ref(_layernorm(x, axis=-1), L1_attn_Wq, L1_attn_Wk, L1_attn_Wv, L1_attn_Wo)
    x = x + _L1_ffn_ref(_layernorm(x, axis=-1), L1_ffn_Wg, L1_ffn_W1, L1_ffn_b1, L1_ffn_W2, L1_ffn_b2)
    return x

_drawn_inputs = setup_inputs


def setup_inputs(seed=0):
    import zlib

    import numpy as np

    out = dict(_drawn_inputs(seed))
    spreads = {'L0_attn_b_qkv': (0.0, 0.353),
     'L0_attn_b_out': (0.0, 0.1),
     'L1_ffn_b1': (0.0, 0.8),
     'L1_ffn_b2': (0.0, 0.8)}
    factors = {'L0_attn_quantum_weights': 8.0,
     'L0_attn_entanglement_gates': 8.0,
     'L0_attn_superposition_logits': 8.0,
     'L1_attn_Wq': 8.0,
     'L1_attn_Wk': 8.0,
     'L1_attn_Wv': 8.0,
     'L1_attn_Wo': 8.0,
     'L1_ffn_Wg': 8.0,
     'L1_ffn_W1': 8.0,
     'L1_ffn_W2': 8.0}
    for name, (base, spread) in spreads.items():
        noise = np.random.default_rng([zlib.crc32(name.encode()), seed]).standard_normal(out[name].shape)
        drawn = base * np.exp(spread * noise) if base else spread * noise
        out[name] = jnp.asarray(drawn.astype(out[name].dtype))
    for name, factor in factors.items():
        out[name] = (out[name] * factor).astype(out[name].dtype)
    return out
```

```python
from contextlib import ExitStack

import concourse.bass as bass
from concourse import mybir

F32 = mybir.dt.float32
BF16 = mybir.dt.bfloat16
U32 = mybir.dt.uint32
I32 = mybir.dt.int32
ALU = mybir.AluOpType
ACT = mybir.ActivationFunctionType
AX = mybir.AxisListType.X

P = 128
T = 2
E = 128
NH, HD = 8, 16
NC = 4
DEPTH = 3
GW = (NH - 1) * HD
HID = 384
NCH = HID // P
H1N, DK = 16, 8
NPAIR = H1N // 2
NX, CAP, FF = 8, 64, 512
NF = FF // P
GRP = 8
EPS = 1e-5
SIGN = 0x80000000
MASKED = -1e30
TWO_PI = 6.283185307179586
PI_HALF = TWO_PI / 4
TURN_HI = 6.28125
TURN_LO = TWO_PI - TURN_HI
ROUND = 12582912.0

ARENA = 28768

DVE_A_STEPS = 41
DVE_B_STEPS = 34


def build(nc, A, out):
    x_in = A["L0_attn_query"]
    B = x_in.shape[0]
    ROWS = min(P, B * NX)
    HALVES = B * NX // ROWS
    NG = B // GRP
    assert B % GRP == 0 and ROWS * HALVES == B * NX

    ctx = ExitStack()
    with ctx:
        def sb(name, shape, dt=F32):
            return ctx.enter_context(nc.sbuf_tensor(name, shape, dt))

        def psum(name, shape, dt=F32):
            return ctx.enter_context(nc.psum_tensor(name, shape, dt))

        sems = {}

        def S(name):
            if name not in sems:
                sems[name] = ctx.enter_context(nc.semaphore(name))
            return sems[name]

        arena = sb("arena", [P, ARENA])

        def carver():
            at = [0]

            def carve(name, shape, dt=F32):
                n = 1
                for s in shape[1:]:
                    n *= s
                words = n if dt != BF16 else n // 2
                a = arena[0:shape[0], at[0]:at[0] + words]
                at[0] += words
                assert at[0] <= ARENA, (name, at[0])
                if dt != F32:
                    a = a.bitcast(dt)
                names = "abcde"[:len(shape) - 1]
                return a if len(shape) == 2 else a.rearrange(
                    f"p ({' '.join(names)}) -> p {' '.join(names)}", **dict(zip(names, shape[1:])))

            return carve

        first, third = carver(), carver()

        x3_d = nc.dram_tensor("x3_scratch", (B, T * P, E), F32, kind="Internal").ap()
        xn4_d = nc.dram_tensor("xn4_scratch", (B, T * P, E), F32, kind="Internal").ap()

        w_qkv_t = sb("w_qkv_t", [P, 3 * E])
        w_out_t = sb("w_out_t", [P, NC, E])
        w_gate_t = sb("w_gate_t", [P, HID])
        w_up_t = sb("w_up_t", [P, HID])
        w_down_t = sb("w_down_t", [P, NCH, E])
        w_l1 = sb("w_l1", [P, 3 * E])
        w_o = sb("w_o", [P, E])
        w_route_t = sb("w_route_t", [P, NX])
        w1 = sb("w1", [P, NX, FF])
        w2 = sb("w2", [P, NX, NF, E])
        b1 = sb("b1", [P, NX, NF])
        b2_row = sb("b2_row", [1, NX, E])
        row = sb("row", [1, 632])
        rows = sb("rows", [P, 632])
        ones_row = sb("ones_row", [1, P])
        ident = sb("ident", [P, P])
        ident_b = sb("ident_b", [P, P], BF16)
        mask_qk = sb("mask_qk", [P, 2, P], BF16)
        mask_kq = sb("mask_kq", [P, 2, P], BF16)
        pick_head = sb("pick_head", [P, H1N, P], BF16)
        slot_ids = sb("slot_ids", [P, CAP])
        neg_half = sb("neg_half", [P, 48])
        spare = sb("spare", [P, 4])
        tiny = sb("tiny", [P, 1])
        c_diag = sb("c_diag", [P, DEPTH, 2, NH * HD])
        c_cross = sb("c_cross", [P, DEPTH, NH * HD])
        g_circuit = sb("g_circuit", [P, NC])
        sup_w = sb("sup_w", [P, NC])
        ph_v = rows[:, 0:16]
        gates_v = rows[:, 16:112].rearrange("p (l i k) -> p l i k", l=DEPTH, i=NH)
        qw_v = rows[:, 112:116]
        sl_v = rows[:, 116:120]
        bqkv_v = rows[:, 120:504]
        bout_row = row[:, 504:632]

        x_land = sb("x_land", [P, T, E])
        x0 = first("x0", [P, T, E])
        x1 = first("x1", [P, T, E])
        stats_a = first("stats_a", [P, T, 6])
        mv_a = first("mv_a", [P, T, 2])
        var_a = first("var_a", [P, T])
        rstd_a = first("rstd_a", [P, T])
        xn_a = first("xn_a", [P, T, E])
        xnt_a = first("xnt_a", [P, T * P])
        qkv = first("qkv", [P, T, 3 * E])
        qkv_sq = first("qkv_sq", [P, T * 3 * E])
        ssq = first("ssq", [P, 48])
        rnorm = first("rnorm", [P, 48])
        state = sb("state", [P, 2, T, 2, E])
        v_enc = first("v_enc", [P, T, E])
        v_sum = first("v_sum", [P, T, HD])
        v_sign = first("v_sign", [P, T, HD], U32)
        gate_sq = first("gate_sq", [P, 2, 4, GW])
        gate_m = first("gate_m", [P, 4, GW])
        gate_p = first("gate_p", [P, 2, 4, GW])
        gate_r = first("gate_r", [P, 2, 4, GW])
        k_both = first("k_both", [P, T, E])
        q_dif = first("q_dif", [P, T, E])
        q_both = first("q_both", [P, T, E])
        gram = first("gram", [P, T, 3, NH * NH])
        pat = first("pat", [P, T, 2, NH * NH])
        pat_sq = first("pat_sq", [P, T, 2, NH * NH])
        pat2 = first("pat2", [P, T, NH * NH])
        pat_max = first("pat_max", [P, T * NH])
        pat_off = first("pat_off", [P, T * NH, NH])
        probs = first("probs", [P, NC * T * NH, NH])
        z_sum = first("z_sum", [P, NC * T * NH])
        z_inv = first("z_inv", [P, NC * T * NH])
        amps = first("amps", [P, NC, T, NH, NH])
        mag = first("mag", [P, T, NC * P])
        clipped = first("clipped", [P, T, NC * P])

        stats_b = first("stats_b", [P, T, 6])
        mv_b = first("mv_b", [P, T, 2])
        var_b = first("var_b", [P, T])
        rstd_b = first("rstd_b", [P, T])
        xn_b = sb("xn_b", [P, T, E])
        xnt_b = first("xnt_b", [P, T * P])
        x2 = first("x2", [P, T, E])
        x3 = sb("x3", [P, T, E])
        tanh_g = first("tanh_g", [P, NCH, T * P])
        hid_t = first("hid_t", [P, NCH, T * P])
        qk32 = first("qk32", [P, 2, T, E])
        qk_res = first("qk_res", [P, 2, T, E])
        qk_p1 = first("qk_p1", [P, 2, T, E], BF16)
        qk_p2 = first("qk_p2", [P, 2, T, E], BF16)
        stack = sb("stack", [P, 2, T * H1N, 8, DK], BF16)
        stack_t = first("stack_t", [P, 2, NPAIR, T * P], BF16)
        v_aug = sb("v_aug", [P, T, H1N, DK + 1])
        s_max = first("s_max", [P, T, H1N])
        s_res = first("s_res", [P, T, H1N])
        max_pad = sb("max_pad", [P, T, P], BF16)
        max_p = max_pad[:, :, 0:3 * H1N].rearrange("p t (h c) -> p t h c", c=3)
        max_t = first("max_t", [P, 3 * P], BF16)
        o_inv = first("o_inv", [P, T * H1N])
        o_n = first("o_n", [P, T, E])
        o_t = first("o_t", [P, T * P])
        r_max = first("r_max", [P, T])
        r_off = first("r_off", [P, T, NX])
        r_exp = first("r_exp", [P, T, NX])
        r_sum = first("r_sum", [P, T])
        r_inv = first("r_inv", [P, T])
        gate_p_all = sb("gate_p_all", [P, T, B * NX])

        prod = first("prod", [P, T, 3, 1024])
        NWP = 3
        wprod = first("wprod", [P, NWP, 1024])
        p_exp = first("p_exp", [P, 2, 2, 384])

        slots = sb("slots", [P, T, B * NX])
        xn_pair = third("xn_pair", [P, 2, T, E])
        x3_pair = third("x3_pair", [P, 2, T, E])
        y_out = third("y_out", [P, 2, T, E])
        onehot = third("onehot", [P, 2, T, NX * CAP])
        onehot_g = third("onehot_g", [P, T, NX, 2 * CAP])
        x_sel = third("x_sel", [P, NX, GRP, CAP])
        h_act = third("h_act", [P, 2, NF, GRP * CAP])
        y_exp = third("y_exp", [P, NX, GRP // 2, E])
        spread_flat = third("spread", [P, GRP // 2 * T * NX * P])
        spread = spread_flat.rearrange("p (m t e n) -> p m t e n", m=GRP // 2, t=T, e=NX)

        start = carver()
        raw = start("raw", [P, 384])
        raw_out = start("raw_out", [P, 128])
        raw_route = start("raw_route", [P, 128])[0:NX, :]
        raw_gate = start("raw_gate", [P, 384])
        raw_up = start("raw_up", [P, 384])
        raw_down = start("raw_down", [P, 384])
        scaled = start("scaled", [P, 384])
        scaled_up = start("scaled_up", [P, 384])
        scaled_down = start("scaled_down", [P, 384])
        ang = start("ang", [P, 836])
        turns = start("turns", [P, 836])
        sines = start("sines", [P, 836])
        tmp = start("tmp", [P, 384])
        wout_s = start("wout_s", [P, 128])
        choice = carver()
        g_rows = choice("g_rows", [P, HALVES, 256])
        g_left = choice("g_left", [P, HALVES, 256])
        g_mask = choice("g_mask", [P, HALVES, 256])
        g_rank = choice("g_rank", [P, HALVES, 256])
        g_one = choice("g_one", [P, 256])
        g_top = choice("g_top", [P, HALVES, 8])

        pa = psum("pa", [P, T, 512])
        pb = psum("pb", [P, 512])
        pc = psum("pc", [P, 512])
        pd = psum("pd", [P, 4, 512])
        pd_b = pd[:, :, :].bitcast(BF16)
        pc_b = pc[:, :].bitcast(BF16)

        def chain(sem, steps):
            n = [0]

            def link(eng, b, ins):
                n[0] += 1
                ins.then_inc(S(sem), 1)
                eng.wait_ge(S(sem), b * steps + n[0])

            return link, n

        def setup_sync(sp):
            def load(dst, src, name="w_in"):
                sp.dma_start(dst, src, allow_slow_non_contiguous=True).then_inc(S(name), 16)

            flat = lambda a, n: A[n].rearrange(a)
            load(row[:, 0:16], flat("a b -> (a b)", "L0_attn_photonic_phases")[0:15 * 129 + 1:129].rearrange("(o n) -> o n", o=1), "row_in")
            load(row[:, 16:112], flat("a b c -> (a b c)", "L0_attn_entanglement_gates").rearrange("(o n) -> o n", o=1), "row_in")
            load(row[:, 112:116], flat("a b c -> (a b c)", "L0_attn_quantum_weights")[0:3 * 64 + 1:64].rearrange("(o n) -> o n", o=1), "row_in")
            load(row[:, 116:120], A["L0_attn_superposition_logits"].rearrange("(o n) -> o n", o=1), "row_in")
            load(row[:, 120:504], A["L0_attn_b_qkv"].rearrange("(o n) -> o n", o=1), "row_in")
            load(row[:, 504:632], A["L0_attn_b_out"].rearrange("(o n) -> o n", o=1), "row_in")
            load(raw[:, 0:384].rearrange("p (c e) -> p c e", c=3), A["L0_attn_W_qkv"].rearrange("(c p) e -> p c e", p=P))
            load(raw_out, A["L0_attn_W_out"])
            load(raw_route, A["L1_ffn_Wg"])
            load(raw_gate.bitcast(I32).rearrange("p (c e) -> p c e", c=3), A["L0_ffn_w_gate"].rearrange("(c p) e -> p c e", p=P))
            load(raw_up.bitcast(I32).rearrange("p (c e) -> p c e", c=3), A["L0_ffn_w_up"].rearrange("(c p) e -> p c e", p=P))
            load(raw_down.bitcast(I32), A["L0_ffn_w_down"])
            load(w_l1[:, 0:128], A["L1_attn_Wq"])
            load(w_l1[:, 128:256], A["L1_attn_Wk"])
            load(w_l1[:, 256:384], A["L1_attn_Wv"])
            load(w_o[:, :], A["L1_attn_Wo"])

        W_IN = 10 * 16

        def setup_scalar_dma(act):
            act.dma_start(w1[:, :, :], A["L1_ffn_W1"].rearrange("e h f -> h e f")).then_inc(S("experts_in"), 16)
            act.dma_start(w2[:, :, :, :], A["L1_ffn_W2"].rearrange("e (c p) h -> p e c h", p=P)).then_inc(S("experts_in"), 16)
            with nc.allow_non_contiguous_dma("4096 single words, once"):
                act.dma_start(b1[:, :, :], A["L1_ffn_b1"].rearrange("e (c p) -> p e c", p=P)).then_inc(S("experts_in"), 16)
            act.dma_start(b2_row[:, :, :], A["L1_ffn_b2"].rearrange("(o e) h -> o e h", o=1)).then_inc(S("experts_in"), 16)

        EXPERTS_IN = 4 * 16

        def setup_gpsimd(g):
            def step(ins):
                ins.then_inc(S("pool_setup"), 1)

            step(g.memset(ident[:, :], 0.0))
            step(g.memset(ident_b[:, :], 0.0))
            step(g.memset(mask_qk[:, :, :], 0.0))
            step(g.memset(mask_kq[:, :, :], 0.0))
            step(g.memset(pick_head[:, :, :], 1.0))
            step(g.memset(neg_half[:, :], -0.5))
            step(g.memset(stack[:, :, :, :, :], 0.0))
            step(g.iota(slot_ids[:, :], [[1, CAP]], base=0, channel_multiplier=0, allow_small_or_imprecise_dtypes=True))
            g.wait_ge(S("pool_setup"), 8)
            for m in (ident, ident_b):
                step(g.affine_select(out=m[:, :], in_=m[:, :], compare_op=ALU.not_equal, fill=1.0, base=0,
                                     pattern=[[-1, P]], channel_multiplier=1))
            step(g.affine_select(out=mask_qk[:, :, :], in_=mask_qk[:, :, :], compare_op=ALU.is_ge, fill=MASKED, base=0,
                                 pattern=[[0, 2], [-1, P]], channel_multiplier=1))
            step(g.affine_select(out=mask_kq[:, :, :], in_=mask_kq[:, :, :], compare_op=ALU.is_ge, fill=MASKED, base=0,
                                 pattern=[[0, 2], [1, P]], channel_multiplier=-1))
            step(g.affine_select(out=pick_head[:, :, :], in_=pick_head[:, :, :], compare_op=ALU.is_ge, fill=0.0, base=0,
                                 pattern=[[-3, H1N], [0, P]], channel_multiplier=1))
            g.wait_ge(S("pool_setup"), 13)
            step(g.affine_select(out=pick_head[:, :, :], in_=pick_head[:, :, :], compare_op=ALU.is_ge, fill=0.0, base=2,
                                 pattern=[[3, H1N], [0, P]], channel_multiplier=-1))
            g.wait_ge(S("pool_setup"), 14)

        POOL_SETUP = 14

        def setup_vector(v):
            n = [0]

            def link(ins):
                n[0] += 1
                ins.then_inc(S("dve_setup"), 1)
                v.wait_ge(S("dve_setup"), n[0])

            link(v.memset(ones_row[:, :], 1.0))
            v.memset(tiny[:, :], 1e-12).then_inc(S("ones_ready"), 1)
            v.memset(v_aug[:, :, :, DK:DK + 1], 1.0).then_inc(S("ones_ready"), 1)
            v.memset(state[:, 1, :, :, :], 0.0).then_inc(S("ones_ready"), 1)
            v.memset(max_pad[:, :, :], 0.0).then_inc(S("ones_ready"), 1)
            v.wait_ge(S("ones_ready"), 4)
            v.wait_ge(S("rows_ps"), 1)
            link(v.tensor_copy(rows[:, 0:504], pa[:, 0, 0:504]))
            link(v.tensor_copy(rows[:, 504:632], pa[:, 1, 0:128]))
            th = gates_v[:, :, :, 0].rearrange("p l i -> p (l i)") if False else gates_v[:, :, :, 0]
            link(v.tensor_scalar(ang[:, 0:24].rearrange("p (l i) -> p l i", l=DEPTH), gates_v[:, :, :, 0], 0.5, None, ALU.mult))
            link(v.tensor_scalar(ang[:, 24:48], ang[:, 0:24], PI_HALF, None, ALU.add))
            link(v.tensor_scalar(tmp[:, 0:16], ph_v, 2.0, None, ALU.mult))
            for l in range(DEPTH):
                link(v.tensor_tensor(ang[:, 48 + 128 * l:176 + 128 * l].rearrange("p (i d) -> p i d", i=NH),
                                     gates_v[:, l, :, 1].unsqueeze(2).broadcast_to([P, NH, HD]),
                                     tmp[:, 0:16].unsqueeze(1).broadcast_to([P, NH, HD]), ALU.subtract))
            link(v.tensor_scalar(ang[:, 432:816], ang[:, 48:432], PI_HALF, None, ALU.add))
            link(v.tensor_scalar(ang[:, 816:832], tmp[:, 0:16], PI_HALF, None, ALU.add))
            link(v.tensor_copy(ang[:, 832:836], qw_v))
            link(v.tensor_scalar(turns, ang, 1.0 / TWO_PI, ROUND, ALU.mult, ALU.add))
            link(v.tensor_scalar(turns, turns, -ROUND, None, ALU.add))
            link(v.scalar_tensor_tensor(ang, turns, -TURN_HI, ang, ALU.mult, ALU.add))
            link(v.scalar_tensor_tensor(ang, turns, -TURN_LO, ang, ALU.mult, ALU.add))
            link(v.tensor_scalar(ang, ang, 3.1415925, -3.1415925, ALU.min, ALU.max))
            v.tensor_copy(tmp[:, 16:20], sl_v).then_inc(S("angles"), 1)
            v.wait_ge(S("sines"), 1)
            sin_h, cos_h = sines[:, 0:24], sines[:, 24:48]
            link(v.tensor_scalar(cos_h, cos_h, -1.0, None, ALU.add))
            for l in range(DEPTH):
                s_b = sin_h[:, 8 * l:8 * l + 8].unsqueeze(2).broadcast_to([P, NH, HD])
                c_b = cos_h[:, 8 * l:8 * l + 8].unsqueeze(2).broadcast_to([P, NH, HD])
                v3 = lambda a: a.rearrange("p (i d) -> p i d", i=NH)
                sin_b, cos_b = v3(sines[:, 48 + 128 * l:176 + 128 * l]), v3(sines[:, 432 + 128 * l:560 + 128 * l])
                link(v.tensor_tensor(v3(c_cross[:, l, :]), sin_b, s_b, ALU.mult))
                link(v.tensor_tensor(cos_b, cos_b, s_b, ALU.mult))
                link(v.tensor_tensor(v3(c_diag[:, l, 0, :]), c_b, cos_b, ALU.add))
                link(v.tensor_tensor(v3(c_diag[:, l, 1, :]), c_b, cos_b, ALU.subtract))
            link(v.tensor_scalar(tmp[:, 32:36], sines[:, 832:836], 0.3, 0.5, ALU.mult, ALU.add))
            link(v.tensor_scalar(tmp[:, 36:40], tmp[:, 32:36], -0.25, 0.25, ALU.mult, ALU.add))
            link(v.tensor_tensor(g_circuit[:, :], tmp[:, 32:36], tmp[:, 36:40], ALU.mult))
            link(v.tensor_reduce(tmp[:, 40:41], sl_v, AX, ALU.max))
            v.tensor_scalar(tmp[:, 44:48], sl_v, tmp[:, 40:41], None, ALU.subtract).then_inc(S("sup_off"), 1)
            v.wait_ge(S("sup_exp"), 1)
            link(v.tensor_reduce(tmp[:, 52:53], tmp[:, 48:52], AX, ALU.add))
            link(v.reciprocal(tmp[:, 53:54], tmp[:, 52:53]))
            link(v.tensor_scalar(sup_w[:, :], tmp[:, 48:52], tmp[:, 53:54], None, ALU.mult))
            v.wait_ge(S("w_in"), W_IN)
            link(v.tensor_tensor(wout_s.rearrange("p (i d) -> p i d", i=NH), raw_out.rearrange("p (i d) -> p i d", i=NH),
                                 sines[:, 816:832].unsqueeze(1).broadcast_to([P, NH, HD]), ALU.mult))
            link(v.tensor_scalar(scaled, raw_gate.bitcast(I32), 1.0 / 127.0, None, ALU.mult))
            link(v.tensor_scalar(scaled_up, raw_up.bitcast(I32), 1.0 / 127.0, None, ALU.mult))
            v.tensor_scalar(scaled_down, raw_down.bitcast(I32), 0.5 / 127.0, None, ALU.mult).then_inc(S("w_scaled"), 1)
            v.wait_ge(S("w_turned"), 1)
            link(v.tensor_copy(w_qkv_t[:, :], pd[:, 0, 0:384]))
            link(v.tensor_copy(w_gate_t[:, :], pd[:, 1, 0:384]))
            link(v.tensor_copy(w_up_t[:, :], pd[:, 2, 0:384]))
            link(v.tensor_copy(w_down_t[:, :, :].rearrange("p c e -> p (c e)"), pd[:, 3, 0:384]))
            link(v.tensor_copy(w_route_t[:, :], pc[:, 0:NX]))
            for c in range(NC):
                link(v.tensor_scalar(w_out_t[:, c, :], pb[:, 0:128], sup_w[:, c:c + 1], None, ALU.mult))
            v.tensor_copy(tmp[:, 0:16], ph_v).then_inc(S("setup_done"), 1)

        def setup_scalar(act):
            act.wait_ge(S("angles"), 1)
            act.activation(sines, ang, ACT.Sin).then_inc(S("sines"), 1)
            act.wait_ge(S("sup_off"), 1)
            act.activation(tmp[:, 48:52], tmp[:, 44:48], ACT.Exp).then_inc(S("sup_exp"), 1)
            act.wait_ge(S("setup_done"), 1)

        def setup_tensor(pe):
            pe.wait_ge(S("row_in"), 6 * 16)
            pe.wait_ge(S("dve_setup"), 1)
            pe.matmul(pa[:, 0, 0:504], ones_row[:, :], row[:, 0:504], start=True, stop=True)
            pe.matmul(pa[:, 1, 0:128], ones_row[:, :], row[:, 504:632], start=True, stop=True).then_inc(S("rows_ps"), 1)
            pe.wait_ge(S("pool_setup"), POOL_SETUP)
            pe.wait_ge(S("w_scaled"), 1)
            for c in range(3):
                cs = slice(c * 128, c * 128 + 128)
                pe.transpose(pd[:, 0, cs], raw[:, cs], ident[:, :])
                pe.transpose(pd[:, 1, cs], scaled[:, cs], ident[:, :])
                pe.transpose(pd[:, 2, cs], scaled_up[:, cs], ident[:, :])
                pe.transpose(pd[:, 3, cs], scaled_down[:, cs], ident[:, :])
            pe.transpose(pb[:, 0:128], wout_s, ident[:, :])
            pe.transpose(pc[:, 0:NX], raw_route, ident[0:NX, 0:NX]).then_inc(S("w_turned"), 1)
            pe.wait_ge(S("setup_done"), 1)

        heads = lambda a, n=NH: a.rearrange("p (i d) -> p i d", d=HD)

        def norm_apply(v, b, src, mv, rstd, dst, done):
            for t in range(T):
                v.tensor_scalar(dst[:, t, :], src[:, t, :], mv[:, t, 0:1], rstd[:, t:t + 1],
                                ALU.subtract, ALU.mult).then_inc(S(done), 1)

        link_a, count_a = chain("dve_a", DVE_A_STEPS)
        link_b, count_b = chain("dve_b", DVE_B_STEPS)

        def vector_a(v, b):
            count_a[0] = 0
            L = lambda ins: link_a(v, b, ins)
            v.wait_ge(S("x_in"), 16 * b + 16)
            for t in range(T):
                count_a[0] += 1
                v.bn_stats(stats_a[:, t, :], x_land[:, t, :]).then_inc(S("dve_a"), 1)
            v.wait_ge(S("dve_a"), b * DVE_A_STEPS + 2)
            v.tensor_copy(x0[:, :, :], x_land[:, :, :]).then_inc(S("x_taken"), 1)
            for t in range(T):
                count_a[0] += 1
                v.bn_aggr(mv_a[:, t, :], stats_a[:, t, :]).then_inc(S("dve_a"), 1)
            v.wait_ge(S("x_taken"), b + 1)
            v.wait_ge(S("dve_a"), b * DVE_A_STEPS + 4)
            v.tensor_scalar(var_a[:, :], mv_a[:, :, 1], EPS, None, ALU.add).then_inc(S("a_var"), 1)
            yield
            v.wait_ge(S("a_rstd"), b + 1)
            norm_apply(v, b, x0, mv_a, rstd_a, xn_a, "a_xn")
            yield
            v.wait_ge(S("a_qkv"), b + 1)
            v.tensor_tensor(qkv[:, :, :], pa[:, :, 0:384], bqkv_v.unsqueeze(1).broadcast_to([P, T, 384]),
                            ALU.add).then_inc(S("a_qkvb"), 1)
            yield
            v.wait_ge(S("a_sq"), b + 1)
            L(v.tensor_reduce(ssq[:, :], qkv_sq[:, :].rearrange("p (g d) -> p g d", d=HD), AX, ALU.add))
            v.tensor_scalar(ssq[:, :], ssq[:, :], 1e-24, None, ALU.max).then_inc(S("a_ssq"), 1)
            yield
            v.wait_ge(S("a_rnorm"), b + 1)
            rn = rnorm[:, :].rearrange("p (t g) -> p t g", t=T)
            q4 = qkv[:, :, :].rearrange("p t (g d) -> p t g d", d=HD)
            v.tensor_tensor(state[:, 0, :, :, :].rearrange("p t k (i d) -> p t (k i) d", d=HD), q4[:, :, 0:16, :],
                            rn[:, :, 0:16].unsqueeze(3).broadcast_to([P, T, 16, HD]), ALU.mult).then_inc(S("a_state"), 1)
            v4 = v_enc[:, :, :].rearrange("p t (i d) -> p t i d", d=HD)
            L(v.tensor_tensor(v4, q4[:, :, 16:24, :], rn[:, :, 16:24].unsqueeze(3).broadcast_to([P, T, 8, HD]), ALU.mult))
            L(v.tensor_reduce(v_sum[:, :, :], v_enc[:, :, :].rearrange("p t (i d) -> p t d i", d=HD), AX, ALU.add))
            L(v.tensor_scalar(v_sign[:, :, :], v_sum[:, :, :].bitcast(U32), SIGN, None, ALU.bitwise_and))
            L(v.tensor_tensor(v4.bitcast(U32), v4.bitcast(U32), v_sign[:, :, :].unsqueeze(2).broadcast_to([P, T, NH, HD]),
                              ALU.bitwise_xor))
            st = state[:, :, :, :, :].rearrange("p c t k n -> p c (t k) n")
            st8 = state[:, :, :, :, :].rearrange("p c t k n -> p (c t k) n")
            g8 = lambda a: a[:, :, :, :].rearrange("p c g n -> p (c g) n")
            cb = lambda a: a.unsqueeze(1).broadcast_to([P, 4, GW])
            v.wait_ge(S("a_state"), 3 * b + 1)
            v.wait_ge(S("a_m"), 3 * b + 1)
            nxt = st[:, 0, :, HD:E]
            L(v.tensor_tensor(gate_m[:, :, :], gate_sq[:, 0, :, :], nxt, ALU.mult))
            L(v.tensor_tensor(gate_p[:, 0, :, :], gate_m[:, :, :], cb(c_diag[:, 0, 0, 0:GW]), ALU.mult))
            L(v.tensor_tensor(st[:, 1, :, 0:GW], gate_m[:, :, :], cb(c_cross[:, 0, 0:GW]), ALU.mult))
            v.tensor_tensor(st[:, 0, :, 0:GW], nxt, gate_p[:, 0, :, :], ALU.add).then_inc(S("a_state"), 1)
            for l in range(1, DEPTH):
                yield
                v.wait_ge(S("a_state"), 3 * b + 1 + l)
                L(v.tensor_tensor(gate_p[:, :, :, :], st[:, :, :, HD:E],
                                  c_diag[:, l, :, 0:GW].unsqueeze(2).broadcast_to([P, 2, 4, GW]), ALU.mult))
                for c in range(2):
                    L(v.tensor_tensor(gate_r[:, c, :, :], st[:, 1 - c, :, HD:E], cb(c_cross[:, l, 0:GW]), ALU.mult))
                L(v.tensor_tensor(g8(gate_p), g8(gate_p), g8(gate_r), ALU.add))
                v.wait_ge(S("a_m"), 3 * b + 1 + l)
                L(v.tensor_tensor(gate_m[:, :, :], gate_sq[:, 0, :, :], gate_sq[:, 1, :, :], ALU.add))
                L(v.tensor_tensor(gate_p[:, :, :, :], gate_p[:, :, :, :],
                                  gate_m[:, :, :].unsqueeze(1).broadcast_to([P, 2, 4, GW]), ALU.mult))
                last = v.tensor_tensor(st8[:, :, 0:GW], st8[:, :, HD:E], g8(gate_p), ALU.add)
                if l < DEPTH - 1:
                    last.then_inc(S("a_state"), 1)
                else:
                    L(last)
            qr, kr = state[:, 0, :, 0, :], state[:, 0, :, 1, :]
            qi, ki = state[:, 1, :, 0, :], state[:, 1, :, 1, :]
            v.tensor_tensor(q_both[:, :, :], qr, qi, ALU.add).then_inc(S("a_pre"), 1)
            L(v.tensor_tensor(k_both[:, :, :], kr, ki, ALU.add))
            L(v.tensor_tensor(q_dif[:, :, :], qr, qi, ALU.subtract))
            for t in range(T):
                yield
                L(v.tensor_tensor(prod4(t, 0), over_j(state[:, 0, t, 0, :]), over_i(k_both[:, t, :]), ALU.mult))
                L(v.tensor_tensor(prod4(t, 1), over_j(q_dif[:, t, :]), over_i(state[:, 1, t, 1, :]), ALU.mult))
                L(v.tensor_reduce(gram[:, t, 0:2, :].rearrange("p k n -> p (k n)"),
                                  prod[:, t, 0:2, :].rearrange("p k (n d) -> p (k n) d", d=HD), AX, ALU.add))
            for t in range(T):
                v.wait_ge(S("a_third"), 2 * b + 1 + t)
                L(v.tensor_reduce(gram[:, t, 2, :], prod[:, t, 2, :].rearrange("p (n d) -> p n d", d=HD), AX, ALU.add))
            v.tensor_tensor(pat[:, :, :, :], gram[:, :, 0:1, :].broadcast_to([P, T, 2, 64]), gram[:, :, 1:3, :],
                            ALU.subtract).then_inc(S("a_pat"), 1)
            yield
            v.wait_ge(S("a_pat_sq"), b + 1)
            L(v.tensor_tensor(pat2[:, :, :], pat_sq[:, :, 0, :], pat_sq[:, :, 1, :], ALU.add))
            p2 = pat2[:, :, :].rearrange("p t (i j) -> p (t i) j", j=NH)
            L(v.tensor_reduce(pat_max[:, :], p2, AX, ALU.max))
            v.tensor_tensor(pat_off[:, :, :], p2, pat_max[:, :].unsqueeze(2).broadcast_to([P, T * NH, NH]),
                            ALU.subtract).then_inc(S("a_off"), 1)
            yield
            v.wait_ge(S("a_exp"), b + 1)
            L(v.tensor_reduce(z_sum[:, :], probs[:, :, :], AX, ALU.add))
            L(v.reciprocal(z_inv[:, :], z_sum[:, :]))
            v.tensor_tensor(probs[:, :, :], probs[:, :, :], z_inv[:, :].unsqueeze(2).broadcast_to([P, NC * T * NH, NH]),
                            ALU.mult).then_inc(S("a_probs"), 1)
            yield
            v.wait_ge(S("a_amps"), b + 1)
            for t in range(T):
                for c in range(NC):
                    k = t * NC + c
                    if k == 4:
                        yield
                    if k >= NWP:
                        v.wait_ge(S("a_wsum"), 8 * b + k - NWP + 1)
                    v.tensor_tensor(wprod[:, k % NWP, :].rearrange("p (j i d) -> p j i d", j=NH, d=HD),
                                    amps[:, c, t, :, :].rearrange("p i j -> p j i").unsqueeze(3).broadcast_to([P, NH, NH, HD]),
                                    v_enc[:, t, :].rearrange("p (j d) -> p j d", d=HD).unsqueeze(2).broadcast_to([P, NH, NH, HD]),
                                    ALU.mult).then_inc(S("a_wprod"), 1)
                    if k == 6:
                        vector_clip(v, b, 0)
            yield
            vector_clip(v, b, 1)
            yield
            v.wait_ge(S("a_y"), b + 1)
            v.tensor_tensor(x1[:, :, :], x0[:, :, :], pb[:, 256:512].rearrange("p (t n) -> p t n", t=T),
                            ALU.add).then_inc(S("x1_ready"), 1)
            assert count_a[0] == DVE_A_STEPS, count_a[0]
            yield

        def prod4(t, k):
            return prod[:, t, k, :].rearrange("p (i j d) -> p i j d", i=NH, d=HD)

        def over_j(a):
            return heads(a).unsqueeze(2).broadcast_to([P, NH, NH, HD])

        def over_i(a):
            return heads(a).unsqueeze(1).broadcast_to([P, NH, NH, HD])

        def vector_clip(v, b, t):
            v.wait_ge(S("a_mag"), 2 * b + t + 1)
            link_a(v, b, v.tensor_scalar(mag[:, t, :], mag[:, t, :], 1e-6, 1.0, ALU.max, ALU.min))
            v.scalar_tensor_tensor(clipped[:, t, :].bitcast(U32), pa[:, t, :].bitcast(U32), SIGN,
                                   mag[:, t, :].bitcast(U32), ALU.bitwise_and, ALU.bitwise_or).then_inc(S("a_clip"), 1)

        def gpsimd_a(g, b):
            g.wait_ge(S("a_var"), b + 1)
            g.tensor_tensor(rstd_a[:, :], var_a[:, :], neg_half[:, 0:2], ALU.pow).then_inc(S("a_rstd"), 1)
            yield
            yield
            yield
            g.wait_ge(S("a_ssq"), b + 1)
            g.tensor_tensor(rnorm[:, :], ssq[:, :], neg_half[:, :], ALU.pow).then_inc(S("a_rnorm"), 1)
            yield
            yield
            yield
            g.wait_ge(S("a_pre"), b + 1)
            yield
            for t in range(T):
                g.tensor_tensor(prod4(t, 2), over_j(q_both[:, t, :]), over_i(state[:, 0, t, 1, :]),
                                ALU.mult).then_inc(S("a_third"), 1)
                yield
            yield
            yield
            for t in range(T):
                for k in range(t * NC, t * NC + NC):
                    g.wait_ge(S("a_wprod"), 8 * b + k + 1)
                    g.tensor_tensor(wprod[:, k % NWP, 0:512], wprod[:, k % NWP, 0:512], wprod[:, k % NWP, 512:1024],
                                    ALU.add).then_inc(S("a_whalf"), 1)
                yield
            yield
            yield

        def scalar_a(act, b):
            yield
            act.wait_ge(S("a_xnt"), b + 1)
            act.activation(xnt_a[:, :], pb[:, 0:256], ACT.Copy).then_inc(S("a_xnts"), 1)
            yield
            act.wait_ge(S("a_qkvb"), b + 1)
            act.activation(qkv_sq[:, :].rearrange("p (t n) -> p t n", t=T), qkv[:, :, :], ACT.Square).then_inc(S("a_sq"), 1)
            yield
            yield
            st = state[:, :, :, :, :].rearrange("p c t k n -> p (c t k) n")
            for l in range(DEPTH):
                n = 4 if l == 0 else 8
                act.wait_ge(S("a_state"), 3 * b + 1 + l)
                act.activation(gate_sq[:, :, :, :].rearrange("p c g n -> p (c g) n")[:, 0:n, :], st[:, 0:n, 0:GW],
                               ACT.Square).then_inc(S("a_m"), 1)
                yield
            yield
            act.wait_ge(S("a_pat"), b + 1)
            act.activation(pat_sq[:, :, :, :], pat[:, :, :, :], ACT.Square).then_inc(S("a_pat_sq"), 1)
            yield
            act.wait_ge(S("a_off"), b + 1)
            for c in range(NC):
                e = act.activation(probs[:, 16 * c:16 * c + 16, :], pat_off[:, :, :], ACT.Exp, scale=g_circuit[:, c:c + 1])
            e.then_inc(S("a_exp"), 1)
            yield
            act.wait_ge(S("a_probs"), b + 1)
            act.activation(amps[:, :, :, :, :].rearrange("p c t i j -> p (c t i) j"), probs[:, :, :], ACT.Sqrt,
                           bias=tiny[:, 0:1]).then_inc(S("a_amps"), 1)
            yield
            yield
            for t in range(T):
                act.wait_ge(S("a_wsum"), 8 * b + 4 * t + 4)
                act.activation(mag[:, t, :], pa[:, t, :], ACT.Abs).then_inc(S("a_mag"), 1)
                yield
            yield

        def tensor_a(pe, b):
            yield
            pe.wait_ge(S("a_xn"), 2 * b + 2)
            pe.transpose(pb[:, 0:128], xn_a[:, 0, :], ident[:, :])
            pe.transpose(pb[:, 128:256], xn_a[:, 1, :], ident[:, :]).then_inc(S("a_xnt"), 1)
            pe.wait_ge(S("a_xnts"), b + 1)
            for t in range(T):
                mm = pe.matmul(pa[:, t, 0:384], xnt_a[:, t * P:t * P + P], w_qkv_t[:, :], start=True, stop=True)
            mm.then_inc(S("a_qkv"), 1)
            for _ in range(10):
                yield
            for t in range(T):
                for c in range(NC):
                    k = t * NC + c
                    pe.wait_ge(S("a_whalf"), 8 * b + k + 1)
                    for j in range(4):
                        mm = pe.matmul(pa[:, t, c * P:c * P + P], wprod[:, k % NWP, j * 128:j * 128 + 128], ident[:, :],
                                       start=(j == 0), stop=(j == 3))
                    mm.then_inc(S("a_wsum"), 1)
                yield
            for t in range(T):
                pe.wait_ge(S("a_clip"), 2 * b + t + 1)
                o = pb[:, 256 + t * 128:384 + t * 128]
                pe.matmul(o, ones_row[:, :], bout_row, start=True, stop=False)
                for c in range(NC):
                    mm = pe.matmul(o, clipped[:, t, c * P:c * P + P], w_out_t[:, c, :], start=False, stop=(c == NC - 1))
            mm.then_inc(S("a_y"), 1)
            yield
            yield

        def vector_norm(v, b, n, src, ready):
            k0 = count_b[0]
            for t in range(T):
                count_b[0] += 1
                v.bn_stats(stats_b[:, t, :], src[:, t, :]).then_inc(S("dve_b"), 1)
            v.wait_ge(S("dve_b"), b * DVE_B_STEPS + k0 + 2)
            v.memset(spare[:, n:n + 1], 0.0).then_inc(S("dve_b"), 1)
            count_b[0] += 1
            for t in range(T):
                count_b[0] += 1
                v.bn_aggr(mv_b[:, t, :], stats_b[:, t, :]).then_inc(S("dve_b"), 1)
            v.wait_ge(S("dve_b"), b * DVE_B_STEPS + k0 + 5)
            v.tensor_scalar(var_b[:, :], mv_b[:, :, 1], EPS, None, ALU.add).then_inc(S("b_var"), 1)
            yield
            v.wait_ge(S("b_rstd"), 3 * b + n + 1)
            if n == 0:
                v.wait_ge(S("xn4_gone"), 16 * b + 1)
            norm_apply(v, b, src, mv_b, rstd_b, xn_b, "b_xn")

        def vector_b(v, b):
            count_b[0] = 0
            L = lambda ins: link_b(v, b, ins)
            v.wait_ge(S("x1_ready"), b + 1)
            yield from vector_norm(v, b, 0, x1, None)
            yield
            for c in range(NCH):
                v.wait_ge(S("b_tanh"), 3 * b + c + 1)
                L(v.scalar_tensor_tensor(tanh_g[:, c, :], tanh_g[:, c, :], 1.0, pd[:, c, 0:256], ALU.add, ALU.mult))
                v.tensor_tensor(hid_t[:, c, :], tanh_g[:, c, :], pd[:, c, 256:512], ALU.mult).then_inc(S("b_hid"), 1)
            yield
            v.wait_ge(S("b_ffn"), b + 1)
            L(v.tensor_tensor(x2[:, :, :], x1[:, :, :], pc[:, 256:512].rearrange("p (t n) -> p t n", t=T), ALU.add))
            yield from vector_norm(v, b, 1, x2, None)
            yield
            flat = lambda a: a[:, :, :, :].rearrange("p k t n -> p (k t n)")
            v.wait_ge(S("b_p1"), b + 1)
            v.tensor_tensor(flat(qk_res), flat(qk32), flat(qk_p1), ALU.subtract).then_inc(S("b_res"), 1)
            yield
            for t in range(T):
                v.wait_ge(S("b_turned"), 4 * b + 2 * t + 2)
                v.tensor_copy(stack_t[:, 1, :, t * P:t * P + P], pd_b[:, 2 * t + 1, :].rearrange("p (h n) -> p h n", n=P))\
                    .then_inc(S("b_kt"), 1)
            yield
            for h in range(NPAIR):
                s = 2 * (h % 2)
                v.wait_ge(S("b_s1"), 8 * b + h + 1)
                count_b[0] += 1
                v.tensor_reduce(s_max[:, 0, 2 * h:2 * h + 2], pd[:, s:s + 2, 0:128], AX, ALU.max).then_inc(S("dve_b"), 1)
                v.tensor_reduce(s_max[:, 1, 2 * h:2 * h + 2], pd[:, s:s + 2, 128:384], AX, ALU.max).then_inc(S("b_m1"), 1)
            v.wait_ge(S("b_m1"), 8 * b + 8)
            L(v.tensor_scalar(max_p[:, :, :, 0], s_max[:, :, :], -1.0, None, ALU.mult))
            L(v.scalar_tensor_tensor(s_res[:, :, :], s_max[:, :, :], -1.0, max_p[:, :, :, 0], ALU.mult, ALU.subtract))
            L(v.tensor_copy(max_p[:, :, :, 1], s_res[:, :, :]))
            v.tensor_tensor(max_p[:, :, :, 2], s_res[:, :, :], max_p[:, :, :, 1], ALU.subtract).then_inc(S("b_mp"), 1)
            yield
            v.wait_ge(S("b_pv"), 8 * b + 8)
            o9 = pc[:, 0:288].rearrange("p (g n) -> p g n", n=DK + 1)
            L(v.reciprocal(o_inv[:, :], o9[:, :, DK]))
            v.tensor_tensor(o_n[:, :, :].rearrange("p t (h d) -> p (t h) d", d=DK), o9[:, :, 0:DK],
                            o_inv[:, :].unsqueeze(2).broadcast_to([P, T * H1N, DK]), ALU.mult).then_inc(S("b_on"), 1)
            yield
            v.wait_ge(S("b_attn"), b + 1)
            v.wait_ge(S("x3_gone"), 16 * b + 1)
            v.tensor_tensor(x3[:, :, :], x2[:, :, :], pd[:, 1, 0:256].rearrange("p (t n) -> p t n", t=T),
                            ALU.add).then_inc(S("x3_ready"), 1)
            v.wait_ge(S("x3_ready"), b + 1)
            yield from vector_norm(v, b, 2, x3, None)
            yield
            lg = pc[:, 256:256 + T * NX].rearrange("p (t e) -> p t e", t=T)
            v.wait_ge(S("b_logits"), b + 1)
            L(v.tensor_reduce(r_max[:, :], lg, AX, ALU.max))
            v.tensor_tensor(r_off[:, :, :], lg, r_max[:, :].unsqueeze(2).broadcast_to([P, T, NX]), ALU.subtract)\
                .then_inc(S("b_roff"), 1)
            yield
            v.wait_ge(S("b_rexp"), b + 1)
            L(v.tensor_reduce(r_sum[:, :], r_exp[:, :, :], AX, ALU.add))
            L(v.reciprocal(r_inv[:, :], r_sum[:, :]))
            v.tensor_tensor(gate_p_all[:, :, bass.ds(b * NX, NX)], r_exp[:, :, :],
                            r_inv[:, :].unsqueeze(2).broadcast_to([P, T, NX]), ALU.mult).then_inc(S("b_gate"), 1)
            assert count_b[0] == DVE_B_STEPS, count_b[0]
            yield

        def gpsimd_norm(g, b, n):
            g.wait_ge(S("b_var"), 3 * b + n + 1)
            g.tensor_tensor(rstd_b[:, :], var_b[:, :], neg_half[:, 0:2], ALU.pow).then_inc(S("b_rstd"), 1)

        def gpsimd_b(g, b):
            gpsimd_norm(g, b, 0)
            yield
            yield
            yield
            gpsimd_norm(g, b, 1)
            yield
            yield
            def part(p, k):
                return p[:, k, :, :].rearrange("p t (h d) -> p (t h) d", d=DK)

            def put(k, first, n, step, p):
                dst = stack[:, k, :, first:first + (n - 1) * step + 1:step, :]
                return g.tensor_copy(dst, part(p, k).unsqueeze(2).broadcast_to([P, T * H1N, n, DK]))

            g.wait_ge(S("b_p2"), b + 1)
            for k, where in ((0, 5), (1, 2)):
                g.tensor_tensor(stack[:, k, :, where, :], part(qk_res, k), part(qk_p2, k), ALU.subtract)
            put(0, 0, 3, 1, qk_p1)
            put(0, 3, 2, 1, qk_p2)
            put(1, 0, 2, 3, qk_p1)
            put(1, 5, 1, 1, qk_p1)
            put(1, 1, 2, 3, qk_p2).then_inc(S("b_stack"), 1)

            for _ in range(4):
                yield
            gpsimd_norm(g, b, 2)
            for _ in range(4):
                yield

        SCALE1 = float(DK) ** -0.5

        def scalar_xnt(act, b, n):
            act.wait_ge(S("b_xnt"), 3 * b + n + 1)
            act.activation(xnt_b[:, :], pc[:, 0:256], ACT.Copy).then_inc(S("b_xnts"), 1)

        def scalar_b(act, b):
            yield
            scalar_xnt(act, b, 0)
            for c in range(NCH):
                act.wait_ge(S("b_gu"), 3 * b + c + 1)
                act.activation(tanh_g[:, c, :], pd[:, c, 0:256], ACT.Tanh, scale=0.5).then_inc(S("b_tanh"), 1)
            yield
            yield
            yield
            scalar_xnt(act, b, 1)
            act.wait_ge(S("b_qkv"), b + 1)
            act.activation(qk32[:, :, :, :].rearrange("p k t n -> p t k n"),
                           pd[:, 0:2, 0:256].rearrange("p t (k n) -> p t k n", k=2), ACT.Copy).then_inc(S("b_qk32"), 1)
            act.activation(v_aug[:, :, :, 0:DK], pd[:, 0:2, 256:384].rearrange("p t (h d) -> p t h d", d=DK),
                           ACT.Copy).then_inc(S("b_v"), 1)
            act.wait_ge(S("b_qk32"), b + 1)
            flat = lambda a: a[:, :, :, :].rearrange("p k t n -> p (k t n)")
            act.activation(flat(qk_p1), flat(qk32), ACT.Copy).then_inc(S("b_p1"), 1)
            yield
            act.wait_ge(S("b_res"), b + 1)
            act.activation(flat(qk_p2), flat(qk_res), ACT.Copy).then_inc(S("b_p2"), 1)
            for t in range(T):
                act.wait_ge(S("b_turned"), 4 * b + 2 * t + 1)
                act.activation(stack_t[:, 0, :, t * P:t * P + P], pd_b[:, 2 * t, :].rearrange("p (h n) -> p h n", n=P),
                               ACT.Copy).then_inc(S("b_qt"), 1)
            yield
            yield
            act.wait_ge(S("b_mt"), b + 1)
            act.activation(max_t[:, 0:256], pc_b[:, 768:1024], ACT.Copy)
            act.activation(max_t[:, 256:384], pc_b[:, 896:1024], ACT.Copy).then_inc(S("b_mts"), 1)
            for h in range(NPAIR):
                s = h % 2
                act.wait_ge(S("b_s2"), 8 * b + h + 1)
                if h >= 2:
                    act.wait_ge(S("b_pv"), 8 * b + h - 1)
                act.activation(p_exp[:, s, :, :], pd[:, 2 * s:2 * s + 2, 0:384], ACT.Exp, scale=SCALE1).then_inc(S("b_e"), 1)
            yield
            act.wait_ge(S("b_ot"), b + 1)
            act.activation(o_t[:, :], pd[:, 0, 0:256], ACT.Copy).then_inc(S("b_ots"), 1)
            yield
            yield
            scalar_xnt(act, b, 2)
            yield
            act.wait_ge(S("b_roff"), b + 1)
            act.activation(r_exp[:, :, :], r_off[:, :, :], ACT.Exp).then_inc(S("b_rexp"), 1)
            yield
            yield

        def tensor_xnt(pe, b, n):
            pe.wait_ge(S("b_xn"), 6 * b + 2 * n + 2)
            pe.transpose(pc[:, 0:128], xn_b[:, 0, :], ident[:, :])
            pe.transpose(pc[:, 128:256], xn_b[:, 1, :], ident[:, :]).then_inc(S("b_xnt"), 1)
            pe.wait_ge(S("b_xnts"), 3 * b + n + 1)

        def tensor_b(pe, b):
            yield
            tensor_xnt(pe, b, 0)
            for c in range(NCH):
                pe.matmul(pd[:, c, 0:256], w_gate_t[:, c * P:c * P + P], xnt_b[:, :], start=True, stop=True)
                pe.matmul(pd[:, c, 256:512], w_up_t[:, c * P:c * P + P], xnt_b[:, :], start=True, stop=True)\
                    .then_inc(S("b_gu"), 1)
            yield
            pe.wait_ge(S("b_hid"), 3 * b + 3)
            for t in range(T):
                for c in range(NCH):
                    mm = pe.matmul(pc[:, 256 + t * P:384 + t * P], hid_t[:, c, t * P:t * P + P], w_down_t[:, c, :],
                                   start=(c == 0), stop=(c == NCH - 1))
            mm.then_inc(S("b_ffn"), 1)
            yield
            yield
            tensor_xnt(pe, b, 1)
            for t in range(T):
                mm = pe.matmul(pd[:, t, 0:384], xnt_b[:, t * P:t * P + P], w_l1[:, :], start=True, stop=True)
            mm.then_inc(S("b_qkv"), 1)
            yield
            pe.wait_ge(S("b_stack"), b + 1)
            pe.wait_ge(S("b_v"), b + 1)
            for r in range(4):
                t, k = r // 2, r % 2
                for h in range(NPAIR):
                    mm = pe.transpose(pd_b[:, r, h * P:h * P + P],
                                      stack[:, k, t * H1N + 2 * h:t * H1N + 2 * h + 2, :, :].rearrange("p g c d -> p (g c d)"),
                                      ident_b[:, :])
                mm.then_inc(S("b_turned"), 1)
            yield
            yield
            pe.wait_ge(S("b_qt"), 2 * b + 2)
            pe.wait_ge(S("b_kt"), 2 * b + 2)

            def qk(k, h, t0, n=1):
                lo = 64 * (h % 2)
                return stack_t[lo:lo + 48, k, h // 2, t0 * P:(t0 + n) * P]

            for h2 in range(NPAIR):
                if h2 >= 2:
                    pe.wait_ge(S("b_m1"), 8 * b + h2 - 1)
                for h in (2 * h2, 2 * h2 + 1):
                    o = pd[:, 2 * (h2 % 2) + h % 2, :]
                    pe.matmul(o[:, 0:256], ident_b[:, :], mask_qk[:, :, :].rearrange("p a n -> p (a n)"), start=True, stop=False,
                              skip_group_check=True)
                    pe.matmul(o[:, 0:128], qk(0, h, 0), qk(1, h, 0), start=False, stop=False, skip_group_check=True)
                    pe.matmul(o[:, 128:256], qk(0, h, 1), qk(1, h, 1), start=False, stop=False, skip_group_check=True)
                    mm = pe.matmul(o[:, 256:384], qk(0, h, 1), qk(1, h, 0), start=False, stop=True, skip_group_check=True)
                mm.then_inc(S("b_s1"), 1)
            pe.wait_ge(S("b_mp"), b + 1)
            for t in range(T):
                mm = pe.transpose(pc_b[:, 768 + t * P:896 + t * P], max_pad[:, t, :], ident_b[:, :])
            mm.then_inc(S("b_mt"), 1)
            pe.wait_ge(S("b_mts"), b + 1)

            def scores(h2):
                if h2 >= 2:
                    pe.wait_ge(S("b_e"), 8 * b + h2 - 1)
                for h in (2 * h2, 2 * h2 + 1):
                    o = pd[:, 2 * (h2 % 2) + h % 2, :]
                    pe.matmul(o[:, 0:256], ident_b[:, :], mask_kq[:, :, :].rearrange("p a n -> p (a n)"), start=True, stop=False,
                              skip_group_check=True)
                    pe.matmul(o[:, 0:384], pick_head[:, h, :], max_t[:, :], start=False, stop=False, skip_group_check=True)
                    pe.matmul(o[:, 0:128], qk(1, h, 0), qk(0, h, 0), start=False, stop=False, skip_group_check=True)
                    pe.matmul(o[:, 256:384], qk(1, h, 0), qk(0, h, 1), start=False, stop=False, skip_group_check=True)
                    mm = pe.matmul(o[:, 128:256], qk(1, h, 1), qk(0, h, 1), start=False, stop=True, skip_group_check=True)
                mm.then_inc(S("b_s2"), 1)

            def values(h2):
                pe.wait_ge(S("b_e"), 8 * b + h2 + 1)
                for h in (2 * h2, 2 * h2 + 1):
                    p = p_exp[:, h2 % 2, h % 2, :]
                    o = lambda t: pc[:, t * 144 + h * 9:t * 144 + h * 9 + 9]
                    pe.matmul(o(0), p[:, 0:128], v_aug[:, 0, h, :], start=True, stop=True, skip_group_check=True)
                    pe.matmul(o(1), p[:, 256:384], v_aug[:, 0, h, :], start=True, stop=False, skip_group_check=True)
                    mm = pe.matmul(o(1), p[:, 128:256], v_aug[:, 1, h, :], start=False, stop=True, skip_group_check=True)
                mm.then_inc(S("b_pv"), 1)

            for h2 in range(NPAIR + 1):
                if h2 < NPAIR:
                    scores(h2)
                if h2 >= 1:
                    values(h2 - 1)
            yield
            pe.wait_ge(S("b_on"), b + 1)
            pe.transpose(pd[:, 0, 0:128], o_n[:, 0, :], ident[:, :])
            pe.transpose(pd[:, 0, 128:256], o_n[:, 1, :], ident[:, :]).then_inc(S("b_ot"), 1)
            pe.wait_ge(S("b_ots"), b + 1)
            for t in range(T):
                mm = pe.matmul(pd[:, 1, t * P:t * P + P], o_t[:, t * P:t * P + P], w_o[:, :], start=True, stop=True)
            mm.then_inc(S("b_attn"), 1)
            yield
            yield
            tensor_xnt(pe, b, 2)
            for t in range(T):
                mm = pe.matmul(pc[:, 256 + t * NX:256 + t * NX + NX], xnt_b[:, t * P:t * P + P], w_route_t[:, :],
                               start=True, stop=True)
            mm.then_inc(S("b_logits"), 1)
            yield
            yield
            yield

        tiles = lambda a: a.rearrange("(t p) e -> p t e", p=P)

        def sync_a(sp, b):
            sp.wait_ge(S("x_taken"), b)
            sp.dma_start(x_land[:, :, :], tiles(x_in[b])).then_inc(S("x_in"), 16)

        def sync_b(sp, b):
            sp.wait_ge(S("x3_ready"), b + 1)
            sp.dma_start(tiles(x3_d[b]), x3[:, :, :]).then_inc(S("x3_gone"), 16)
            sp.wait_ge(S("b_xn"), 6 * b + 6)
            sp.dma_start(tiles(xn4_d[b]), xn_b[:, :, :]).then_inc(S("xn4_gone"), 16)

        def vector_choose(v):
            n = [0]

            def link(ins):
                n[0] += 1
                ins.then_inc(S("dve_choose"), 1)
                v.wait_ge(S("dve_choose"), n[0])

            v.wait_ge(S("rows_turned"), 1)
            R = ROWS
            for h in range(HALVES):
                link(v.tensor_copy(g_rows[0:R, h, :], pd[0:R, h, 0:256]))
            link(v.memset(g_one, 1.0))
            src = g_rows
            for k in range(CAP // 8):
                for h in range(HALVES):
                    v.max(g_top[0:R, h, :], src[0:R, h, :]).then_inc(S("dve_choose"), 1)
                    n[0] += 1
                v.wait_ge(S("dve_choose"), n[0])
                for h in range(HALVES):
                    v.match_replace(g_left[0:R, h, :], g_top[0:R, h, :], src[0:R, h, :], -1.0).then_inc(S("dve_choose"), 1)
                    n[0] += 1
                v.wait_ge(S("dve_choose"), n[0])
                src = g_left
            for h in range(HALVES):
                link(v.tensor_scalar(g_mask[0:R, h, :], g_left[0:R, h, :], 0.0, None, ALU.is_lt))
                link(v.tensor_tensor_scan(g_rank[0:R, h, :], g_one[0:R, :], g_mask[0:R, h, :], 0.0, ALU.mult, ALU.add))
                link(v.tensor_tensor(g_rank[0:R, h, :], g_rank[0:R, h, :], g_mask[0:R, h, :], ALU.mult))
                link(v.tensor_scalar(g_rank[0:R, h, :], g_rank[0:R, h, :], -1.0, None, ALU.add))
            v.tensor_copy(g_top[0:R, 0, 0:1], g_one[0:R, 0:1]).then_inc(S("ranks"), 1)
            v.wait_ge(S("slots_turned"), 1)
            for t in range(T):
                for h in range(HALVES):
                    link(v.tensor_copy(slots[:, t, h * R:h * R + R], pd[:, 2 + t, h * 128:h * 128 + R]))
            v.tensor_copy(spare[:, 3:4], g_one[:, 0:1]).then_inc(S("chosen"), 1)
            v.wait_ge(S("chosen"), 1)

        def tensor_choose(pe):
            pe.wait_ge(S("b_gate"), B)
            R = ROWS
            for h in range(HALVES):
                for t in range(T):
                    mm = pe.transpose(pd[0:R, h, t * P:t * P + P], gate_p_all[:, t, h * R:h * R + R], ident[:, :])
            mm.then_inc(S("rows_turned"), 1)
            pe.wait_ge(S("ranks"), 1)
            for t in range(T):
                for h in range(HALVES):
                    mm = pe.transpose(pd[:, 2 + t, h * 128:h * 128 + R], g_rank[0:R, h, t * P:t * P + P], ident[0:R, 0:R])
            mm.then_inc(S("slots_turned"), 1)

        NM = GRP // 2

        def sync_experts(sp, g):
            for m in range(NM):
                sp.wait_ge(S("c_sel"), GRP * g + 2 * m + 1)
                sp.dma_start(xn_pair[:, :, :, :].rearrange("p b t e -> p (b t) e"),
                             pairs(xn4_d, g, m)).then_inc(S("c_xn_in"), 16)
            for m in range(NM):
                sp.wait_ge(S("c_added"), NM * g + m + 1)
                sp.dma_start(x3_pair[:, :, :, :].rearrange("p b t e -> p (b t) e"), pairs(x3_d, g, m)).then_inc(S("c_x3_in"), 16)
                sp.wait_ge(S("c_added"), NM * g + m + 2)
                sp.dma_start(pairs(out, g, m), y_out[:, :, :, :].rearrange("p b t e -> p (b t) e")).then_inc(S("out_gone"), 16)

        def pairs(d, g, m):
            flat = d.rearrange("b (t p) e -> p (b t) e", p=P)
            return flat[:, bass.ds(g * (GRP * T) + m * 2 * T, 2 * T), :]

        def oh(a, b):
            return a[:, b, :, :].rearrange("p t (e s) -> p t e s", s=CAP)

        def vector_experts(v, g):
            for m in range(NM):
                v.wait_ge(S("c_sel"), GRP * g + 2 * m + 1)
                v.wait_ge(S("c_turned"), 4 * NM * g + 4 * m + 1)
                for b in range(2):
                    col = g * (GRP * NX) + (2 * m + b) * NX
                    where = slots[:, :, bass.ds(col, NX)].unsqueeze(3).broadcast_to([P, T, NX, CAP])
                    weight = gate_p_all[:, :, bass.ds(col, NX)].unsqueeze(3).broadcast_to([P, T, NX, CAP])
                    v.tensor_tensor(oh(onehot, b), slot_ids[:, :].unsqueeze(1).unsqueeze(1).broadcast_to([P, T, NX, CAP]),
                                    where, ALU.is_equal).then_inc(S("c_onehot"), 1)
                    v.wait_ge(S("c_onehot"), 2 * NM * g + 2 * m + b + 1)
                    v.tensor_tensor(onehot_g[:, :, :, b * CAP:b * CAP + CAP], oh(onehot, b), weight, ALU.mult).then_inc(S("c_weighted"), 1)
                for k in range(4):
                    v.wait_ge(S("c_turned"), 4 * NM * g + 4 * m + k + 2)
                    v.tensor_copy(spread_flat[:, m * 2048 + k * 512:m * 2048 + k * 512 + 512], pd[:, k, :]).then_inc(S("c_spread"), 1)
            for e in range(NX):
                v.wait_ge(S("c_y"), NX * g + e + 1)
                v.tensor_copy(y_exp[:, e, :, :].rearrange("p m n -> p (m n)"), pa[:, e % 2, :]).then_inc(S("c_yexp"), 1)
            for m in range(NM):
                v.wait_ge(S("c_x3_in"), 16 * (NM * g + m) + 16)
                v.wait_ge(S("c_scattered"), NM * g + m + 1)
                v.wait_ge(S("out_gone"), 16 * (NM * g + m) + 1)
                for b, bank in enumerate((pc, pb)):
                    y = v.tensor_tensor(y_out[:, b, :, :].rearrange("p t e -> p (t e)"),
                                        x3_pair[:, b, :, :].rearrange("p t e -> p (t e)"), bank[:, 0:256], ALU.add)
                y.then_inc(S("c_added"), 1)

        def scalar_experts(act, g):
            for m in range(NM):
                for b in range(2):
                    act.wait_ge(S("c_sel"), GRP * g + 2 * m + b + 2)
                    act.activation(x_sel[:, :, 2 * m + b, :], pa[:, b, :].rearrange("p (e s) -> p e s", s=CAP),
                                   ACT.Copy).then_inc(S("c_xsel"), 1)
            for e in range(NX):
                for f in range(NF):
                    act.wait_ge(S("c_h"), NX * NF * g + NF * e + f + 1)
                    if f == 0 and e >= 2:
                        act.wait_ge(S("c_y"), NX * g + e - 1)
                    act.activation(h_act[:, e % 2, f, :], pd[:, f, :], ACT.Gelu_apprx_tanh, bias=b1[:, e, f:f + 1])\
                        .then_inc(S("c_gelu"), 1)

        def tensor_experts(pe, g):
            for m in range(NM):
                pe.wait_ge(S("c_xn_in"), 16 * (NM * g + m) + 16)
                pe.wait_ge(S("c_onehot"), 2 * NM * g + 2 * m + 2)
                for b in range(2):
                    if m:
                        pe.wait_ge(S("c_xsel"), GRP * g + 2 * m + b - 1)
                    for t in range(T):
                        mm = pe.matmul(pa[:, b, :], xn_pair[:, b, t, :], onehot[:, b, t, :],
                                       start=(t == 0), stop=(t == T - 1))
                    mm.then_inc(S("c_sel"), 1)
                pe.wait_ge(S("c_weighted"), 2 * NM * g + 2 * m + 2)
                if m:
                    pe.wait_ge(S("c_spread"), 4 * NM * g + 4 * m)
                for k in range(4):
                    for j in range(4):
                        t, e = divmod(4 * k + j, NX)
                        mm = pe.transpose(pd[:, k, j * P:j * P + P], onehot_g[:, t, e, :], ident[:, :])
                    mm.then_inc(S("c_turned"), 1)
            pe.wait_ge(S("c_xsel"), GRP * g + GRP)
            pe.wait_ge(S("c_spread"), 4 * NM * g + 4 * NM)

            def up(e):
                for f in range(NF):
                    if e:
                        pe.wait_ge(S("c_gelu"), NX * NF * g + NF * (e - 1) + f + 1)
                    pe.matmul(pd[:, f, :], w1[:, e, f * P:f * P + P], x_sel[:, e, :, :].rearrange("p b s -> p (b s)"),
                              start=True, stop=True).then_inc(S("c_h"), 1)

            def down(e):
                pe.wait_ge(S("c_gelu"), NX * NF * g + NF * e + NF)
                if e >= 2:
                    pe.wait_ge(S("c_yexp"), NX * g + e - 1)
                for m in range(NM):
                    o = pa[:, e % 2, m * E:m * E + E]
                    pe.matmul(o, ones_row[:, :], b2_row[:, e, :], start=True, stop=False)
                    for f in range(NF):
                        mm = pe.matmul(o, h_act[:, e % 2, f, m * P:m * P + P], w2[:, e, f, :], start=False, stop=(f == NF - 1))
                mm.then_inc(S("c_y"), 1)

            for e in range(NX + 1):
                if e < NX:
                    up(e)
                if e:
                    down(e - 1)
            pe.wait_ge(S("c_yexp"), NX * g + NX)
            for m in range(NM):
                pe.wait_ge(S("c_added"), NM * g + m + 1)
                for t in range(T):
                    for e in range(NX):
                        for b, bank in enumerate((pc, pb)):
                            lo = b * CAP
                            mm = pe.matmul(bank[:, t * E:t * E + E], spread[lo:lo + CAP, m, t, e, :],
                                           y_exp[lo:lo + CAP, e, m, :], start=(e == 0), stop=(e == NX - 1))
                mm.then_inc(S("c_scattered"), 1)

        ORDER = "ABABAABBABABABBAAABABABABABA"

        def both(stage_a, stage_b, eng, b):
            run = {"A": stage_a(eng, b), "B": stage_b(eng, b - 1)}
            for s in ORDER:
                next(run[s])

        def alone(stage, eng, b):
            pieces = sum(1 for _ in stage(eng, b))
            assert pieces == ORDER.count("A" if b == 0 else "B"), pieces

        def sequences(stage_a, stage_b, eng):
            alone(stage_a, eng, 0)
            with eng.Fori(1, B) as b:
                both(stage_a, stage_b, eng, b)
            alone(stage_b, eng, B - 1)

        block = ctx.enter_context(nc.Block())

        @block.sync
        def _(sp):
            setup_sync(sp)
            sp.dma_start(x_land[:, :, :], tiles(x_in[0])).then_inc(S("x_in"), 16)
            with sp.Fori(1, B) as b:
                sync_a(sp, b)
                sync_b(sp, b - 1)
            sync_b(sp, B - 1)
            sp.wait_ge(S("x3_gone"), 16 * B + 1)
            sp.wait_ge(S("xn4_gone"), 16 * B + 1)
            sp.wait_ge(S("chosen"), 1)
            with sp.Fori(0, NG) as g:
                sync_experts(sp, g)
            sp.wait_ge(S("out_gone"), 16 * NM * NG + 1)

        @block.gpsimd
        def _(g):
            setup_gpsimd(g)
            sequences(gpsimd_a, gpsimd_b, g)

        @block.scalar
        def _(act):
            setup_scalar_dma(act)
            setup_scalar(act)
            act.wait_ge(S("pool_setup"), POOL_SETUP)
            sequences(scalar_a, scalar_b, act)
            act.wait_ge(S("experts_in"), EXPERTS_IN)
            with act.Fori(0, NG) as g:
                scalar_experts(act, g)

        @block.tensor
        def _(pe):
            setup_tensor(pe)
            sequences(tensor_a, tensor_b, pe)
            tensor_choose(pe)
            pe.wait_ge(S("experts_in"), EXPERTS_IN)
            with pe.Fori(0, NG) as g:
                tensor_experts(pe, g)

        @block.vector
        def _(v):
            setup_vector(v)
            for name in ("x3_gone", "xn4_gone", "c_sel", "c_added", "c_turned", "out_gone"):
                v.sem_inc(S(name), 1)
            v.wait_ge(S("pool_setup"), POOL_SETUP)
            sequences(vector_a, vector_b, v)
            vector_choose(v)
            with v.Fori(0, NG) as g:
                vector_experts(v, g)


_INS = ["L0_attn_query", "L0_attn_W_qkv", "L0_attn_b_qkv", "L0_attn_W_out", "L0_attn_b_out",
        "L0_attn_quantum_weights", "L0_attn_photonic_phases", "L0_attn_entanglement_gates",
        "L0_attn_superposition_logits", "L0_ffn_w_gate", "L0_ffn_w_up", "L0_ffn_w_down",
        "L1_attn_Wq", "L1_attn_Wk", "L1_attn_Wv", "L1_attn_Wo",
        "L1_ffn_Wg", "L1_ffn_W1", "L1_ffn_b1", "L1_ffn_W2", "L1_ffn_b2"]


def kernel(**inputs):
    import numpy as _np
    import concourse.bacc as _bacc
    from concourse import mybir as _mybir
    from concourse.bass_utils import run_bass_kernel_spmd as _run

    nc = _bacc.Bacc("TRN2", target_bir_lowering=False, num_devices=1)
    arrays, args = {}, {}
    for name in _INS:
        a = _np.ascontiguousarray(inputs[name])
        arrays[f"in_{name}"] = a
        args[name] = nc.dram_tensor(f"in_{name}", a.shape, _mybir.dt.from_np(a.dtype), kind="ExternalInput").ap()
    shape = inputs["L0_attn_query"].shape
    out = nc.dram_tensor("out_x", shape, _mybir.dt.float32, kind="ExternalOutput").ap()
    build(nc, args, out)
    r = _run(nc, [arrays], core_ids=[0])
    return r.results[0]["out_x"]
```

```python
from contextlib import ExitStack

import concourse.bass as bass
from concourse import mybir

F32 = mybir.dt.float32
BF16 = mybir.dt.bfloat16
U32 = mybir.dt.uint32
I32 = mybir.dt.int32
ALU = mybir.AluOpType
ACT = mybir.ActivationFunctionType
AX = mybir.AxisListType.X

P = 128
T = 2
E = 128
NH, HD = 8, 16
NC = 4
DEPTH = 3
GW = (NH - 1) * HD
HID = 384
NCH = HID // P
H1N, DK = 16, 8
NPAIR = H1N // 2
NX, CAP, FF = 8, 64, 512
NF = FF // P
GRP = 8
EPS = 1e-5
SIGN = 0x80000000
MASKED = -1e30
TWO_PI = 6.283185307179586
PI_HALF = TWO_PI / 4
TURN_HI = 6.28125
TURN_LO = TWO_PI - TURN_HI
ROUND = 12582912.0

ARENA = 28768

DVE_A_STEPS = 35
DVE_B_STEPS = 34

POOL_ORDER = "A1B1A2B1A4B3A10B1"
ACT_ORDER = "A1B1A1B3A2B3A1B9A1B2A1B1A1B3A1B2A1B2"
PE_ORDER = "A1B1A1B35A3B1A1B1A1B1A1B2A3B2A1"
DVE_ORDER = "A3B3A1B1A3B9A1B1A4B1A4B1A8B14A25B2A1B5A2B5A1"


def build(nc, A, out):
    x_in = A["L0_attn_query"]
    B = x_in.shape[0]
    ROWS = min(P, B * NX)
    HALVES = B * NX // ROWS
    NG = B // GRP
    assert B % GRP == 0 and ROWS * HALVES == B * NX

    ctx = ExitStack()
    with ctx:
        def sb(name, shape, dt=F32):
            return ctx.enter_context(nc.sbuf_tensor(name, shape, dt))

        def psum(name, shape, dt=F32):
            return ctx.enter_context(nc.psum_tensor(name, shape, dt))

        sems = {}

        def S(name):
            if name not in sems:
                sems[name] = ctx.enter_context(nc.semaphore(name))
            return sems[name]

        arena = sb("arena", [P, ARENA])

        def carver():
            at = [0]

            def carve(name, shape, dt=F32):
                n = 1
                for s in shape[1:]:
                    n *= s
                words = n if dt != BF16 else n // 2
                a = arena[0:shape[0], at[0]:at[0] + words]
                at[0] += words
                assert at[0] <= ARENA, (name, at[0])
                if dt != F32:
                    a = a.bitcast(dt)
                names = "abcde"[:len(shape) - 1]
                return a if len(shape) == 2 else a.rearrange(
                    f"p ({' '.join(names)}) -> p {' '.join(names)}", **dict(zip(names, shape[1:])))

            return carve

        first, third = carver(), carver()

        x3_d = nc.dram_tensor("x3_scratch", (B, T * P, E), F32, kind="Internal").ap()
        xn4_d = nc.dram_tensor("xn4_scratch", (B, T * P, E), F32, kind="Internal").ap()

        w_qkv_t = sb("w_qkv_t", [P, 3 * E])
        w_out_t = sb("w_out_t", [P, NC, E])
        w_gate_t = sb("w_gate_t", [P, HID])
        w_up_t = sb("w_up_t", [P, HID])
        w_down_t = sb("w_down_t", [P, NCH, E])
        w_l1 = sb("w_l1", [P, 3 * E])
        w_o = sb("w_o", [P, E])
        w_route_t = sb("w_route_t", [P, NX])
        w1 = sb("w1", [P, NX, FF])
        w2 = sb("w2", [P, NX, NF, E])
        b1 = sb("b1", [P, NX, NF])
        b2_row = sb("b2_row", [1, NX, E])
        row = sb("row", [1, 632])
        rows = sb("rows", [P, 632])
        ones_row = sb("ones_row", [1, P])
        ident = sb("ident", [P, P])
        ident_b = sb("ident_b", [P, P], BF16)
        mask_qk = sb("mask_qk", [P, 2, P], BF16)
        mask_kq = sb("mask_kq", [P, 2, P], BF16)
        pick_head = sb("pick_head", [P, H1N, P], BF16)
        slot_ids = sb("slot_ids", [P, CAP])
        neg_half = sb("neg_half", [P, 48])
        spare = sb("spare", [P, 4])
        tiny = sb("tiny", [P, 1])
        c_diag = sb("c_diag", [P, DEPTH, 2, NH * HD])
        c_cross = sb("c_cross", [P, DEPTH, NH * HD])
        g_circuit = sb("g_circuit", [P, NC])
        sup_w = sb("sup_w", [P, NC])
        ph_v = rows[:, 0:16]
        gates_v = rows[:, 16:112].rearrange("p (l i k) -> p l i k", l=DEPTH, i=NH)
        qw_v = rows[:, 112:116]
        sl_v = rows[:, 116:120]
        bqkv_v = rows[:, 120:504]
        bout_row = row[:, 504:632]

        x_land = sb("x_land", [P, T, E])
        x0 = first("x0", [P, T, E])
        x1 = first("x1", [P, T, E])
        stats_a = first("stats_a", [P, T, 6])
        mv_a = first("mv_a", [P, T, 2])
        var_a = first("var_a", [P, T])
        rstd_a = first("rstd_a", [P, T])
        xn_a = first("xn_a", [P, T, E])
        xnt_a = first("xnt_a", [P, T * P])
        qkv = first("qkv", [P, T, 3 * E])
        qkv_sq = first("qkv_sq", [P, T * 3 * E])
        ssq = first("ssq", [P, 48])
        rnorm = first("rnorm", [P, 48])
        state = sb("state", [P, 2, T, 2, E])
        v_enc = first("v_enc", [P, T, E])
        v_sum = first("v_sum", [P, T, HD])
        v_sign = first("v_sign", [P, T, HD], U32)
        gate_sq = first("gate_sq", [P, 2, 4, GW])
        gate_m = first("gate_m", [P, 4, GW])
        gate_p = first("gate_p", [P, 2, 4, GW])
        gate_r = first("gate_r", [P, 2, 4, GW])
        k_both = first("k_both", [P, T, E])
        q_dif = first("q_dif", [P, T, E])
        q_both = first("q_both", [P, T, E])
        gram = first("gram", [P, T, 3, NH * NH])
        pat = first("pat", [P, T, 2, NH * NH])
        pat_sq = first("pat_sq", [P, T, 2, NH * NH])
        pat2 = first("pat2", [P, T, NH * NH])
        pat_max = first("pat_max", [P, T * NH])
        pat_off = first("pat_off", [P, T * NH, NH])
        probs = first("probs", [P, NC * T * NH, NH])
        z_sum = first("z_sum", [P, NC * T * NH])
        z_inv = first("z_inv", [P, NC * T * NH])
        amps = first("amps", [P, NC, T, NH, NH])
        mag = first("mag", [P, T, NC * P])
        clipped = first("clipped", [P, T, NC * P])

        stats_b = first("stats_b", [P, T, 6])
        mv_b = first("mv_b", [P, T, 2])
        var_b = first("var_b", [P, T])
        rstd_b = first("rstd_b", [P, T])
        xn_b = sb("xn_b", [P, T, E])
        xnt_b = first("xnt_b", [P, T * P])
        x2 = first("x2", [P, T, E])
        x3 = sb("x3", [P, T, E])
        tanh_g = first("tanh_g", [P, NCH, T * P])
        hid_t = first("hid_t", [P, NCH, T * P])
        o_raw = hid_t[:, 0:2, :].rearrange("p c n -> p (c n)")
        qk32 = first("qk32", [P, 2, T, E])
        qk_res = first("qk_res", [P, 2, T, E])
        qk_p1 = first("qk_p1", [P, 2, T, E], BF16)
        qk_p2 = first("qk_p2", [P, 2, T, E], BF16)
        stack = sb("stack", [P, 2, T * H1N, 8, DK], BF16)
        stack_t = first("stack_t", [P, 2, NPAIR, T * P], BF16)
        HG, VW = H1N // 2, 8 * DK + 8
        v_pad = sb("v_pad", [P, T * 2, HG * (VW + DK)])
        v_own = v_pad[:, :, :].rearrange("p a (j w) -> p a j w", w=VW + DK)[:, :, :, 0:DK]
        s_max = first("s_max", [P, T, H1N])
        s_res = first("s_res", [P, T, H1N])
        max_pad = sb("max_pad", [P, T, P], BF16)
        max_p = max_pad[:, :, 0:3 * H1N].rearrange("p t (h c) -> p t h c", c=3)
        max_t = first("max_t", [P, 3 * P], BF16)
        o_inv = first("o_inv", [P, T * H1N])
        o_n = first("o_n", [P, T, E])
        o_t = first("o_t", [P, T * P])
        r_max = first("r_max", [P, T])
        r_off = first("r_off", [P, T, NX])
        r_exp = first("r_exp", [P, T, NX])
        r_sum = first("r_sum", [P, T])
        r_inv = first("r_inv", [P, T])
        gate_p_all = sb("gate_p_all", [P, T, B * NX])

        prod = first("prod", [P, T, 3, 1024])
        NWP = 3
        wprod = first("wprod", [P, NWP, 1024])
        p_exp = first("p_exp", [P, 2, 2, 384])

        slots = sb("slots", [P, T, B * NX])
        xn_pair = [third(f"xn_pair_{i}", [P, 2, T, E]) for i in range(2)]
        x3_pair = [third(f"x3_pair_{i}", [P, 2, T, E]) for i in range(2)]
        y_out = [third(f"y_out_{i}", [P, 2, T, E]) for i in range(2)]
        onehot_0 = third("onehot", [P, 2 * T * NX * CAP])
        weighted_0 = third("weighted", [P, T * NX * 2 * CAP])
        x_sel = third("x_sel", [P, NX, GRP, CAP])
        h_flat = third("h_act", [P, 2 * NF * GRP * CAP])
        h_act = h_flat.rearrange("p (a f n) -> p a f n", a=2, f=NF)
        HALF = 2 * T * NX * CAP
        onehot = [a.rearrange("p (b t n) -> p b t n", b=2, t=T) for a in (onehot_0, h_flat[:, 0:HALF])]
        weighted = [a.rearrange("p (t e n) -> p t e n", t=T, e=NX) for a in (weighted_0, h_flat[:, HALF:2 * HALF])]
        y_exp = third("y_exp", [P, NX, GRP // 2, E])
        spread_flat = third("spread", [P, GRP // 2 * T * NX * P])
        spread = spread_flat.rearrange("p (m t e n) -> p m t e n", m=GRP // 2, t=T, e=NX)

        start = carver()
        raw = start("raw", [P, 384])
        raw_out = start("raw_out", [P, 128])
        raw_route = start("raw_route", [P, 128])[0:NX, :]
        raw_gate = start("raw_gate", [P, 384])
        raw_up = start("raw_up", [P, 384])
        raw_down = start("raw_down", [P, 384])
        scaled = start("scaled", [P, 384])
        scaled_up = start("scaled_up", [P, 384])
        scaled_down = start("scaled_down", [P, 384])
        ang = start("ang", [P, 836])
        turns = start("turns", [P, 836])
        sines = start("sines", [P, 836])
        tmp = start("tmp", [P, 384])
        wout_s = start("wout_s", [P, 128])
        choice = carver()
        g_rows = choice("g_rows", [P, HALVES, 256])
        g_left = choice("g_left", [P, HALVES, 256])
        g_mask = choice("g_mask", [P, HALVES, 256])
        g_rank = choice("g_rank", [P, HALVES, 256])
        g_one = choice("g_one", [P, 256])
        g_top = choice("g_top", [P, HALVES, 8])

        pa = psum("pa", [P, T, 512])
        pb = psum("pb", [P, 512])
        pc = psum("pc", [P, 512])
        pd = psum("pd", [P, 4, 512])
        pd_b = pd[:, :, :].bitcast(BF16)
        pc_b = pc[:, :].bitcast(BF16)

        def chain(sem, steps):
            n = [0]

            def link(eng, b, ins):
                n[0] += 1
                k = n[0]
                ins.then_inc(S(sem), 1)
                yield
                eng.wait_ge(S(sem), b * steps + k)

            return link, n

        def setup_sync(sp):
            def load(dst, src, name="w_in"):
                sp.dma_start(dst, src, allow_slow_non_contiguous=True).then_inc(S(name), 16)

            flat = lambda a, n: A[n].rearrange(a)
            load(row[:, 0:16], flat("a b -> (a b)", "L0_attn_photonic_phases")[0:15 * 129 + 1:129].rearrange("(o n) -> o n", o=1), "row_in")
            load(row[:, 16:112], flat("a b c -> (a b c)", "L0_attn_entanglement_gates").rearrange("(o n) -> o n", o=1), "row_in")
            load(row[:, 112:116], flat("a b c -> (a b c)", "L0_attn_quantum_weights")[0:3 * 64 + 1:64].rearrange("(o n) -> o n", o=1), "row_in")
            load(row[:, 116:120], A["L0_attn_superposition_logits"].rearrange("(o n) -> o n", o=1), "row_in")
            load(row[:, 120:504], A["L0_attn_b_qkv"].rearrange("(o n) -> o n", o=1), "row_in")
            load(row[:, 504:632], A["L0_attn_b_out"].rearrange("(o n) -> o n", o=1), "row_in")
            load(raw[:, 0:384].rearrange("p (c e) -> p c e", c=3), A["L0_attn_W_qkv"].rearrange("(c p) e -> p c e", p=P))
            load(raw_out, A["L0_attn_W_out"])
            load(raw_route, A["L1_ffn_Wg"])
            load(raw_gate.bitcast(I32).rearrange("p (c e) -> p c e", c=3), A["L0_ffn_w_gate"].rearrange("(c p) e -> p c e", p=P))
            load(raw_up.bitcast(I32).rearrange("p (c e) -> p c e", c=3), A["L0_ffn_w_up"].rearrange("(c p) e -> p c e", p=P))
            load(raw_down.bitcast(I32), A["L0_ffn_w_down"])
            load(w_l1[:, 0:128], A["L1_attn_Wq"])
            load(w_l1[:, 128:256], A["L1_attn_Wk"])
            load(w_l1[:, 256:384], A["L1_attn_Wv"])
            load(w_o[:, :], A["L1_attn_Wo"])

        W_IN = 10 * 16

        def setup_scalar_dma(act):
            act.dma_start(w1[:, :, :], A["L1_ffn_W1"].rearrange("e h f -> h e f")).then_inc(S("experts_in"), 16)
            act.dma_start(w2[:, :, :, :], A["L1_ffn_W2"].rearrange("e (c p) h -> p e c h", p=P)).then_inc(S("experts_in"), 16)
            with nc.allow_non_contiguous_dma("4096 single words, once"):
                act.dma_start(b1[:, :, :], A["L1_ffn_b1"].rearrange("e (c p) -> p e c", p=P)).then_inc(S("experts_in"), 16)
            act.dma_start(b2_row[:, :, :], A["L1_ffn_b2"].rearrange("(o e) h -> o e h", o=1)).then_inc(S("experts_in"), 16)

        EXPERTS_IN = 4 * 16

        def setup_gpsimd(g):
            def step(ins):
                ins.then_inc(S("pool_setup"), 1)

            step(g.memset(ident[:, :], 0.0))
            step(g.memset(ident_b[:, :], 0.0))
            step(g.memset(mask_qk[:, :, :], 0.0))
            step(g.memset(mask_kq[:, :, :], 0.0))
            step(g.memset(pick_head[:, :, :], 1.0))
            step(g.memset(neg_half[:, :], -0.5))
            step(g.memset(stack[:, :, :, :, :], 0.0))
            step(g.iota(slot_ids[:, :], [[1, CAP]], base=0, channel_multiplier=0, allow_small_or_imprecise_dtypes=True))
            g.wait_ge(S("pool_setup"), 8)
            for m in (ident, ident_b):
                step(g.affine_select(out=m[:, :], in_=m[:, :], compare_op=ALU.not_equal, fill=1.0, base=0,
                                     pattern=[[-1, P]], channel_multiplier=1))
            step(g.affine_select(out=mask_qk[:, :, :], in_=mask_qk[:, :, :], compare_op=ALU.is_ge, fill=MASKED, base=0,
                                 pattern=[[0, 2], [-1, P]], channel_multiplier=1))
            step(g.affine_select(out=mask_kq[:, :, :], in_=mask_kq[:, :, :], compare_op=ALU.is_ge, fill=MASKED, base=0,
                                 pattern=[[0, 2], [1, P]], channel_multiplier=-1))
            step(g.affine_select(out=pick_head[:, :, :], in_=pick_head[:, :, :], compare_op=ALU.is_ge, fill=0.0, base=0,
                                 pattern=[[-3, H1N], [0, P]], channel_multiplier=1))
            g.wait_ge(S("pool_setup"), 13)
            step(g.affine_select(out=pick_head[:, :, :], in_=pick_head[:, :, :], compare_op=ALU.is_ge, fill=0.0, base=2,
                                 pattern=[[3, H1N], [0, P]], channel_multiplier=-1))
            g.wait_ge(S("pool_setup"), 14)

        POOL_SETUP = 14

        def setup_vector(v):
            n = [0]

            def link(ins):
                n[0] += 1
                ins.then_inc(S("dve_setup"), 1)
                v.wait_ge(S("dve_setup"), n[0])

            link(v.memset(ones_row[:, :], 1.0))
            v.memset(tiny[:, :], 1e-12).then_inc(S("ones_ready"), 1)
            v.memset(v_pad[:, :, :], 0.0).then_inc(S("ones_ready"), 1)
            v.memset(state[:, 1, :, :, :], 0.0).then_inc(S("ones_ready"), 1)
            v.memset(max_pad[:, :, :], 0.0).then_inc(S("ones_ready"), 1)
            v.wait_ge(S("ones_ready"), 4)
            for j in range(HG):
                one = j * VW + HG * DK + j
                link(v.memset(v_pad[:, :, one:one + 1], 1.0))
            v.wait_ge(S("rows_ps"), 1)
            link(v.tensor_copy(rows[:, 0:504], pa[:, 0, 0:504]))
            link(v.tensor_copy(rows[:, 504:632], pa[:, 1, 0:128]))
            th = gates_v[:, :, :, 0]
            link(v.tensor_scalar(ang[:, 0:24].rearrange("p (l i) -> p l i", l=DEPTH), gates_v[:, :, :, 0], 0.5, None, ALU.mult))
            link(v.tensor_scalar(ang[:, 24:48], ang[:, 0:24], PI_HALF, None, ALU.add))
            link(v.tensor_scalar(tmp[:, 0:16], ph_v, 2.0, None, ALU.mult))
            for l in range(DEPTH):
                link(v.tensor_tensor(ang[:, 48 + 128 * l:176 + 128 * l].rearrange("p (i d) -> p i d", i=NH),
                                     gates_v[:, l, :, 1].unsqueeze(2).broadcast_to([P, NH, HD]),
                                     tmp[:, 0:16].unsqueeze(1).broadcast_to([P, NH, HD]), ALU.subtract))
            link(v.tensor_scalar(ang[:, 432:816], ang[:, 48:432], PI_HALF, None, ALU.add))
            link(v.tensor_scalar(ang[:, 816:832], tmp[:, 0:16], PI_HALF, None, ALU.add))
            link(v.tensor_copy(ang[:, 832:836], qw_v))
            link(v.tensor_scalar(turns, ang, 1.0 / TWO_PI, ROUND, ALU.mult, ALU.add))
            link(v.tensor_scalar(turns, turns, -ROUND, None, ALU.add))
            link(v.scalar_tensor_tensor(ang, turns, -TURN_HI, ang, ALU.mult, ALU.add))
            link(v.scalar_tensor_tensor(ang, turns, -TURN_LO, ang, ALU.mult, ALU.add))
            link(v.tensor_scalar(ang, ang, 3.1415925, -3.1415925, ALU.min, ALU.max))
            v.tensor_copy(tmp[:, 16:20], sl_v).then_inc(S("angles"), 1)
            v.wait_ge(S("sines"), 1)
            sin_h, cos_h = sines[:, 0:24], sines[:, 24:48]
            link(v.tensor_scalar(cos_h, cos_h, -1.0, None, ALU.add))
            for l in range(DEPTH):
                s_b = sin_h[:, 8 * l:8 * l + 8].unsqueeze(2).broadcast_to([P, NH, HD])
                c_b = cos_h[:, 8 * l:8 * l + 8].unsqueeze(2).broadcast_to([P, NH, HD])
                v3 = lambda a: a.rearrange("p (i d) -> p i d", i=NH)
                sin_b, cos_b = v3(sines[:, 48 + 128 * l:176 + 128 * l]), v3(sines[:, 432 + 128 * l:560 + 128 * l])
                link(v.tensor_tensor(v3(c_cross[:, l, :]), sin_b, s_b, ALU.mult))
                link(v.tensor_tensor(cos_b, cos_b, s_b, ALU.mult))
                link(v.tensor_tensor(v3(c_diag[:, l, 0, :]), c_b, cos_b, ALU.add))
                link(v.tensor_tensor(v3(c_diag[:, l, 1, :]), c_b, cos_b, ALU.subtract))
            link(v.tensor_scalar(tmp[:, 32:36], sines[:, 832:836], 0.3, 0.5, ALU.mult, ALU.add))
            link(v.tensor_scalar(tmp[:, 36:40], tmp[:, 32:36], -0.25, 0.25, ALU.mult, ALU.add))
            link(v.tensor_tensor(g_circuit[:, :], tmp[:, 32:36], tmp[:, 36:40], ALU.mult))
            link(v.tensor_reduce(tmp[:, 40:41], sl_v, AX, ALU.max))
            v.tensor_scalar(tmp[:, 44:48], sl_v, tmp[:, 40:41], None, ALU.subtract).then_inc(S("sup_off"), 1)
            v.wait_ge(S("sup_exp"), 1)
            link(v.tensor_reduce(tmp[:, 52:53], tmp[:, 48:52], AX, ALU.add))
            link(v.reciprocal(tmp[:, 53:54], tmp[:, 52:53]))
            link(v.tensor_scalar(sup_w[:, :], tmp[:, 48:52], tmp[:, 53:54], None, ALU.mult))
            v.wait_ge(S("w_in"), W_IN)
            link(v.tensor_tensor(wout_s.rearrange("p (i d) -> p i d", i=NH), raw_out.rearrange("p (i d) -> p i d", i=NH),
                                 sines[:, 816:832].unsqueeze(1).broadcast_to([P, NH, HD]), ALU.mult))
            link(v.tensor_scalar(scaled, raw_gate.bitcast(I32), 1.0 / 127.0, None, ALU.mult))
            link(v.tensor_scalar(scaled_up, raw_up.bitcast(I32), 1.0 / 127.0, None, ALU.mult))
            v.tensor_scalar(scaled_down, raw_down.bitcast(I32), 0.5 / 127.0, None, ALU.mult).then_inc(S("w_scaled"), 1)
            v.wait_ge(S("w_turned"), 1)
            link(v.tensor_copy(w_qkv_t[:, :], pd[:, 0, 0:384]))
            link(v.tensor_copy(w_gate_t[:, :], pd[:, 1, 0:384]))
            link(v.tensor_copy(w_up_t[:, :], pd[:, 2, 0:384]))
            link(v.tensor_copy(w_down_t[:, :, :].rearrange("p c e -> p (c e)"), pd[:, 3, 0:384]))
            link(v.tensor_copy(w_route_t[:, :], pc[:, 0:NX]))
            for c in range(NC):
                link(v.tensor_scalar(w_out_t[:, c, :], pb[:, 0:128], sup_w[:, c:c + 1], None, ALU.mult))
            v.tensor_copy(tmp[:, 0:16], ph_v).then_inc(S("setup_done"), 1)

        def setup_scalar(act):
            act.wait_ge(S("angles"), 1)
            act.activation(sines, ang, ACT.Sin).then_inc(S("sines"), 1)
            act.wait_ge(S("sup_off"), 1)
            act.activation(tmp[:, 48:52], tmp[:, 44:48], ACT.Exp).then_inc(S("sup_exp"), 1)
            act.wait_ge(S("setup_done"), 1)

        def setup_tensor(pe):
            pe.wait_ge(S("row_in"), 6 * 16)
            pe.wait_ge(S("dve_setup"), 1)
            pe.matmul(pa[:, 0, 0:504], ones_row[:, :], row[:, 0:504], start=True, stop=True)
            pe.matmul(pa[:, 1, 0:128], ones_row[:, :], row[:, 504:632], start=True, stop=True).then_inc(S("rows_ps"), 1)
            pe.wait_ge(S("pool_setup"), POOL_SETUP)
            pe.wait_ge(S("w_scaled"), 1)
            for c in range(3):
                cs = slice(c * 128, c * 128 + 128)
                pe.transpose(pd[:, 0, cs], raw[:, cs], ident[:, :])
                pe.transpose(pd[:, 1, cs], scaled[:, cs], ident[:, :])
                pe.transpose(pd[:, 2, cs], scaled_up[:, cs], ident[:, :])
                pe.transpose(pd[:, 3, cs], scaled_down[:, cs], ident[:, :])
            pe.transpose(pb[:, 0:128], wout_s, ident[:, :])
            pe.transpose(pc[:, 0:NX], raw_route, ident[0:NX, 0:NX]).then_inc(S("w_turned"), 1)
            pe.wait_ge(S("setup_done"), 1)

        heads = lambda a, n=NH: a.rearrange("p (i d) -> p i d", d=HD)

        def norm_apply(v, src, mv, rstd, dst, done):
            for t in range(T):
                v.tensor_scalar(dst[:, t, :], src[:, t, :], mv[:, t, 0:1], rstd[:, t:t + 1],
                                ALU.subtract, ALU.mult).then_inc(S(done), 1)

        link_a, count_a = chain("dve_a", DVE_A_STEPS)
        link_b, count_b = chain("dve_b", DVE_B_STEPS)

        def vector_a(v, b):
            count_a[0] = 0
            L = lambda ins: link_a(v, b, ins)
            v.wait_ge(S("x_in"), 16 * b + 16)
            for t in range(T):
                count_a[0] += 1
                v.bn_stats(stats_a[:, t, :], x_land[:, t, :]).then_inc(S("dve_a"), 1)
            yield
            v.wait_ge(S("dve_a"), b * DVE_A_STEPS + 2)
            v.tensor_copy(x0[:, :, :], x_land[:, :, :]).then_inc(S("x_taken"), 1)
            for t in range(T):
                count_a[0] += 1
                v.bn_aggr(mv_a[:, t, :], stats_a[:, t, :]).then_inc(S("dve_a"), 1)
            yield
            v.wait_ge(S("x_taken"), b + 1)
            v.wait_ge(S("dve_a"), b * DVE_A_STEPS + 4)
            v.tensor_scalar(var_a[:, :], mv_a[:, :, 1], EPS, None, ALU.add).then_inc(S("a_var"), 1)
            yield
            v.wait_ge(S("a_rstd"), b + 1)
            norm_apply(v, x0, mv_a, rstd_a, xn_a, "a_xn")
            yield
            v.wait_ge(S("a_qkv"), b + 1)
            v.tensor_tensor(qkv[:, :, :], pa[:, :, 0:384], bqkv_v.unsqueeze(1).broadcast_to([P, T, 384]),
                            ALU.add).then_inc(S("a_qkvb"), 1)
            yield
            v.wait_ge(S("a_sq"), b + 1)
            yield from L(v.tensor_reduce(ssq[:, :], qkv_sq[:, :].rearrange("p (g d) -> p g d", d=HD), AX, ALU.add))
            v.tensor_scalar(ssq[:, :], ssq[:, :], 1e-24, None, ALU.max).then_inc(S("a_ssq"), 1)
            yield
            v.wait_ge(S("a_rnorm"), 2 * b + 1)
            rn = rnorm[:, :].rearrange("p (t g) -> p t g", t=T)
            q4 = qkv[:, :, :].rearrange("p t (g d) -> p t g d", d=HD)
            v.tensor_tensor(state[:, 0, :, :, :].rearrange("p t k (i d) -> p t (k i) d", d=HD), q4[:, :, 0:16, :],
                            rn[:, :, 0:16].unsqueeze(3).broadcast_to([P, T, 16, HD]), ALU.mult).then_inc(S("a_state"), 1)
            st = state[:, :, :, :, :].rearrange("p c t k n -> p c (t k) n")
            st8 = state[:, :, :, :, :].rearrange("p c t k n -> p (c t k) n")
            g8 = lambda a: a[:, :, :, :].rearrange("p c g n -> p (c g) n")
            cb = lambda a: a.unsqueeze(1).broadcast_to([P, 4, GW])
            v.wait_ge(S("a_state"), 3 * b + 1)
            v.wait_ge(S("a_m"), 3 * b + 1)
            nxt = st[:, 0, :, HD:E]
            yield from L(v.tensor_tensor(gate_m[:, :, :], gate_sq[:, 0, :, :], nxt, ALU.mult))
            yield from L(v.tensor_tensor(gate_p[:, 0, :, :], gate_m[:, :, :], cb(c_diag[:, 0, 0, 0:GW]), ALU.mult))
            yield from L(v.tensor_tensor(st[:, 1, :, 0:GW], gate_m[:, :, :], cb(c_cross[:, 0, 0:GW]), ALU.mult))
            v.tensor_tensor(st[:, 0, :, 0:GW], nxt, gate_p[:, 0, :, :], ALU.add).then_inc(S("a_state"), 1)
            for l in range(1, DEPTH):
                yield
                v.wait_ge(S("a_state"), 3 * b + 1 + l)
                yield from L(v.tensor_tensor(gate_p[:, :, :, :], st[:, :, :, HD:E],
                                  c_diag[:, l, :, 0:GW].unsqueeze(2).broadcast_to([P, 2, 4, GW]), ALU.mult))
                v.wait_ge(S("a_cross"), 2 * b + l)
                yield from L(v.tensor_tensor(g8(gate_p), g8(gate_p), g8(gate_r), ALU.add))
                v.wait_ge(S("a_ctrl"), 2 * b + l)
                yield from L(v.tensor_tensor(gate_p[:, :, :, :], gate_p[:, :, :, :],
                                  gate_m[:, :, :].unsqueeze(1).broadcast_to([P, 2, 4, GW]), ALU.mult))
                last = v.tensor_tensor(st8[:, :, 0:GW], st8[:, :, HD:E], g8(gate_p), ALU.add)
                if l < DEPTH - 1:
                    last.then_inc(S("a_state"), 1)
                else:
                    yield from L(last)
            qr, kr = state[:, 0, :, 0, :], state[:, 0, :, 1, :]
            qi, ki = state[:, 1, :, 0, :], state[:, 1, :, 1, :]
            v.tensor_tensor(q_both[:, :, :], qr, qi, ALU.add).then_inc(S("a_pre"), 1)
            yield from L(v.tensor_tensor(k_both[:, :, :], kr, ki, ALU.add))
            yield from L(v.tensor_tensor(q_dif[:, :, :], qr, qi, ALU.subtract))
            for t in range(T):
                yield from L(v.tensor_tensor(prod4(t, 0), over_j(state[:, 0, t, 0, :]), over_i(k_both[:, t, :]), ALU.mult))
                yield from L(v.tensor_tensor(prod4(t, 1), over_j(q_dif[:, t, :]), over_i(state[:, 1, t, 1, :]), ALU.mult))
                yield from L(v.tensor_reduce(gram[:, t, 0:2, :].rearrange("p k n -> p (k n)"),
                                  prod[:, t, 0:2, :].rearrange("p k (n d) -> p (k n) d", d=HD), AX, ALU.add))
            for t in range(T):
                v.wait_ge(S("a_third"), 2 * b + 1 + t)
                yield from L(v.tensor_reduce(gram[:, t, 2, :], prod[:, t, 2, :].rearrange("p (n d) -> p n d", d=HD), AX, ALU.add))
            v.tensor_tensor(pat[:, :, :, :], gram[:, :, 0:1, :].broadcast_to([P, T, 2, 64]), gram[:, :, 1:3, :],
                            ALU.subtract).then_inc(S("a_pat"), 1)
            yield
            v4 = v_enc[:, :, :].rearrange("p t (i d) -> p t i d", d=HD)
            v.wait_ge(S("a_rnorm"), 2 * b + 2)
            yield from L(v.tensor_tensor(v4, q4[:, :, 16:24, :], rn[:, :, 16:24].unsqueeze(3).broadcast_to([P, T, 8, HD]), ALU.mult))
            yield from L(v.tensor_reduce(v_sum[:, :, :], v_enc[:, :, :].rearrange("p t (i d) -> p t d i", d=HD), AX, ALU.add))
            v.wait_ge(S("a_pat_sq"), b + 1)
            yield from L(v.tensor_tensor(pat2[:, :, :], pat_sq[:, :, 0, :], pat_sq[:, :, 1, :], ALU.add))
            p2 = pat2[:, :, :].rearrange("p t (i j) -> p (t i) j", j=NH)
            yield from L(v.tensor_reduce(pat_max[:, :], p2, AX, ALU.max))
            v.tensor_tensor(pat_off[:, :, :], p2, pat_max[:, :].unsqueeze(2).broadcast_to([P, T * NH, NH]),
                            ALU.subtract).then_inc(S("a_off"), 1)
            yield
            yield from L(v.tensor_scalar(v_sign[:, :, :], v_sum[:, :, :].bitcast(U32), SIGN, None, ALU.bitwise_and))
            yield from L(v.tensor_tensor(v4.bitcast(U32), v4.bitcast(U32), v_sign[:, :, :].unsqueeze(2).broadcast_to([P, T, NH, HD]),
                                         ALU.bitwise_xor))
            v.wait_ge(S("a_exp"), b + 1)
            yield from L(v.tensor_reduce(z_sum[:, :], probs[:, :, :], AX, ALU.add))
            yield from L(v.reciprocal(z_inv[:, :], z_sum[:, :]))
            v.tensor_tensor(probs[:, :, :], probs[:, :, :], z_inv[:, :].unsqueeze(2).broadcast_to([P, NC * T * NH, NH]),
                            ALU.mult).then_inc(S("a_probs"), 1)
            yield
            v.wait_ge(S("a_amps"), b + 1)
            for t in range(T):
                for c in range(NC):
                    k = t * NC + c
                    if k:
                        yield
                    if k >= NWP:
                        v.wait_ge(S("a_wsum"), 8 * b + k - NWP + 1)
                    v.tensor_tensor(wprod[:, k % NWP, :].rearrange("p (j i d) -> p j i d", j=NH, d=HD),
                                    amps[:, c, t, :, :].rearrange("p i j -> p j i").unsqueeze(3).broadcast_to([P, NH, NH, HD]),
                                    v_enc[:, t, :].rearrange("p (j d) -> p j d", d=HD).unsqueeze(2).broadcast_to([P, NH, NH, HD]),
                                    ALU.mult).then_inc(S("a_wprod"), 1)
                    if k == 6:
                        yield
                        yield from vector_clip(v, b, 0)
            yield
            yield from vector_clip(v, b, 1)
            yield
            v.wait_ge(S("a_y"), b + 1)
            if not isinstance(b, int):
                v.wait_ge(S("b_var"), 3 * b - 1)
            v.tensor_tensor(x1[:, :, :], x0[:, :, :], pb[:, 256:512].rearrange("p (t n) -> p t n", t=T),
                            ALU.add).then_inc(S("x1_ready"), 1)
            assert count_a[0] == DVE_A_STEPS, count_a[0]
            yield

        def prod4(t, k):
            return prod[:, t, k, :].rearrange("p (i j d) -> p i j d", i=NH, d=HD)

        def over_j(a):
            return heads(a).unsqueeze(2).broadcast_to([P, NH, NH, HD])

        def over_i(a):
            return heads(a).unsqueeze(1).broadcast_to([P, NH, NH, HD])

        def vector_clip(v, b, t):
            v.wait_ge(S("a_mag"), 2 * b + t + 1)
            yield from link_a(v, b, v.tensor_scalar(mag[:, t, :], mag[:, t, :], 1e-6, 1.0, ALU.max, ALU.min))
            v.scalar_tensor_tensor(clipped[:, t, :].bitcast(U32), pa[:, t, :].bitcast(U32), SIGN,
                                   mag[:, t, :].bitcast(U32), ALU.bitwise_and, ALU.bitwise_or).then_inc(S("a_clip"), 1)

        def gpsimd_a(g, b):
            g.wait_ge(S("a_var"), b + 1)
            g.tensor_tensor(rstd_a[:, :], var_a[:, :], neg_half[:, 0:2], ALU.pow).then_inc(S("a_rstd"), 1)
            yield
            g.wait_ge(S("a_ssq"), b + 1)
            of_tile = lambda a: a[:, :].rearrange("p (t n) -> p t n", t=T)
            for c in (slice(0, 16), slice(16, 24)):
                g.tensor_tensor(of_tile(rnorm)[:, :, c], of_tile(ssq)[:, :, c], of_tile(neg_half)[:, :, c],
                                ALU.pow).then_inc(S("a_rnorm"), 1)
                yield
            st = state[:, :, :, :, :].rearrange("p c t k n -> p c (t k) n")
            for l in range(1, DEPTH):
                g.wait_ge(S("a_state"), 3 * b + 1 + l)
                for c in range(2):
                    ins = g.tensor_tensor(gate_r[:, c, :, :], st[:, 1 - c, :, HD:E],
                                          c_cross[:, l, 0:GW].unsqueeze(1).broadcast_to([P, 4, GW]), ALU.mult)
                ins.then_inc(S("a_cross"), 1)
                yield
                g.wait_ge(S("a_m"), 3 * b + 1 + l)
                g.tensor_tensor(gate_m[:, :, :], gate_sq[:, 0, :, :], gate_sq[:, 1, :, :], ALU.add).then_inc(S("a_ctrl"), 1)
                yield
            for t in range(T):
                if t == 0:
                    g.wait_ge(S("a_pre"), b + 1)
                g.tensor_tensor(prod4(t, 2), over_j(q_both[:, t, :]), over_i(state[:, 0, t, 1, :]),
                                ALU.mult).then_inc(S("a_third"), 1)
                yield
            for t in range(T):
                for k in range(t * NC, t * NC + NC):
                    if k % NC:
                        yield
                    g.wait_ge(S("a_wprod"), 8 * b + k + 1)
                    g.tensor_tensor(wprod[:, k % NWP, 0:512], wprod[:, k % NWP, 0:512], wprod[:, k % NWP, 512:1024],
                                    ALU.add).then_inc(S("a_whalf"), 1)
                yield

        def scalar_a(act, b):
            act.wait_ge(S("a_xnt"), b + 1)
            act.activation(xnt_a[:, :], pb[:, 0:256], ACT.Copy).then_inc(S("a_xnts"), 1)
            yield
            act.wait_ge(S("a_qkvb"), b + 1)
            act.activation(qkv_sq[:, :].rearrange("p (t n) -> p t n", t=T), qkv[:, :, :], ACT.Square).then_inc(S("a_sq"), 1)
            yield
            st = state[:, :, :, :, :].rearrange("p c t k n -> p (c t k) n")
            for l in range(DEPTH):
                n = 4 if l == 0 else 8
                act.wait_ge(S("a_state"), 3 * b + 1 + l)
                act.activation(gate_sq[:, :, :, :].rearrange("p c g n -> p (c g) n")[:, 0:n, :], st[:, 0:n, 0:GW],
                               ACT.Square).then_inc(S("a_m"), 1)
                yield
            act.wait_ge(S("a_pat"), b + 1)
            act.activation(pat_sq[:, :, :, :], pat[:, :, :, :], ACT.Square).then_inc(S("a_pat_sq"), 1)
            yield
            act.wait_ge(S("a_off"), b + 1)
            for c in range(NC):
                e = act.activation(probs[:, 16 * c:16 * c + 16, :], pat_off[:, :, :], ACT.Exp, scale=g_circuit[:, c:c + 1])
            e.then_inc(S("a_exp"), 1)
            yield
            act.wait_ge(S("a_probs"), b + 1)
            act.activation(amps[:, :, :, :, :].rearrange("p c t i j -> p (c t i) j"), probs[:, :, :], ACT.Sqrt,
                           bias=tiny[:, 0:1]).then_inc(S("a_amps"), 1)
            yield
            for t in range(T):
                act.wait_ge(S("a_wsum"), 8 * b + 4 * t + 4)
                act.activation(mag[:, t, :], pa[:, t, :], ACT.Abs).then_inc(S("a_mag"), 1)
                yield

        def tensor_a(pe, b):
            pe.wait_ge(S("a_xn"), 2 * b + 2)
            pe.transpose(pb[:, 0:128], xn_a[:, 0, :], ident[:, :])
            pe.transpose(pb[:, 128:256], xn_a[:, 1, :], ident[:, :]).then_inc(S("a_xnt"), 1)
            yield
            pe.wait_ge(S("a_xnts"), b + 1)
            for t in range(T):
                mm = pe.matmul(pa[:, t, 0:384], xnt_a[:, t * P:t * P + P], w_qkv_t[:, :], start=True, stop=True)
            mm.then_inc(S("a_qkv"), 1)
            for t in range(T):
                for c in range(NC):
                    k = t * NC + c
                    yield
                    pe.wait_ge(S("a_whalf"), 8 * b + k + 1)
                    for j in range(4):
                        mm = pe.matmul(pa[:, t, c * P:c * P + P], wprod[:, k % NWP, j * 128:j * 128 + 128], ident[:, :],
                                       start=(j == 0), stop=(j == 3))
                    mm.then_inc(S("a_wsum"), 1)
            for t in range(T):
                yield
                pe.wait_ge(S("a_clip"), 2 * b + t + 1)
                o = pb[:, 256 + t * 128:384 + t * 128]
                pe.matmul(o, ones_row[:, :], bout_row, start=True, stop=False)
                for c in range(NC):
                    mm = pe.matmul(o, clipped[:, t, c * P:c * P + P], w_out_t[:, c, :], start=False, stop=(c == NC - 1))
            mm.then_inc(S("a_y"), 1)
            yield

        def vector_norm(v, b, n, src):
            k0 = count_b[0]
            for t in range(T):
                count_b[0] += 1
                v.bn_stats(stats_b[:, t, :], src[:, t, :]).then_inc(S("dve_b"), 1)
            yield
            v.wait_ge(S("dve_b"), b * DVE_B_STEPS + k0 + 2)
            v.memset(spare[:, n:n + 1], 0.0).then_inc(S("dve_b"), 1)
            count_b[0] += 1
            for t in range(T):
                count_b[0] += 1
                v.bn_aggr(mv_b[:, t, :], stats_b[:, t, :]).then_inc(S("dve_b"), 1)
            yield
            v.wait_ge(S("dve_b"), b * DVE_B_STEPS + k0 + 5)
            v.tensor_scalar(var_b[:, :], mv_b[:, :, 1], EPS, None, ALU.add).then_inc(S("b_var"), 1)
            yield
            v.wait_ge(S("b_rstd"), 3 * b + n + 1)
            if n == 0:
                v.wait_ge(S("xn4_gone"), 16 * b + 1)
            norm_apply(v, src, mv_b, rstd_b, xn_b, "b_xn")

        def vector_b(v, b):
            count_b[0] = 0
            L = lambda ins: link_b(v, b, ins)
            v.wait_ge(S("x1_ready"), b + 1)
            yield from vector_norm(v, b, 0, x1)
            yield
            for c in range(NCH):
                if c:
                    yield
                v.wait_ge(S("b_tanh"), 3 * b + c + 1)
                yield from L(v.scalar_tensor_tensor(tanh_g[:, c, :], tanh_g[:, c, :], 1.0, pd[:, c, 0:256], ALU.add, ALU.mult))
                v.tensor_tensor(hid_t[:, c, :], tanh_g[:, c, :], pd[:, c, 256:512], ALU.mult).then_inc(S("b_hid"), 1)
            yield
            v.wait_ge(S("b_ffn"), b + 1)
            yield from L(v.tensor_tensor(x2[:, :, :], x1[:, :, :], pc[:, 256:512].rearrange("p (t n) -> p t n", t=T), ALU.add))
            yield from vector_norm(v, b, 1, x2)
            yield
            flat = lambda a: a[:, :, :, :].rearrange("p k t n -> p (k t n)")
            v.wait_ge(S("b_p1"), b + 1)
            v.tensor_tensor(flat(qk_res), flat(qk32), flat(qk_p1), ALU.subtract).then_inc(S("b_res"), 1)
            yield
            for t in range(T):
                if t:
                    yield
                v.wait_ge(S("b_turned"), 4 * b + 2 * t + 2)
                v.tensor_copy(stack_t[:, 1, :, t * P:t * P + P], pd_b[:, 2 * t + 1, :].rearrange("p (h n) -> p h n", n=P))\
                    .then_inc(S("b_kt"), 1)
            yield
            for h in range(NPAIR):
                s = 2 * (h % 2)
                if h:
                    yield
                v.wait_ge(S("b_s1"), 8 * b + h + 1)
                count_b[0] += 1
                v.tensor_reduce(s_max[:, 0, 2 * h:2 * h + 2], pd[:, s:s + 2, 0:128], AX, ALU.max).then_inc(S("dve_b"), 1)
                v.tensor_reduce(s_max[:, 1, 2 * h:2 * h + 2], pd[:, s:s + 2, 128:384], AX, ALU.max).then_inc(S("b_m1"), 1)
            yield
            v.wait_ge(S("b_m1"), 8 * b + 8)
            yield from L(v.tensor_scalar(max_p[:, :, :, 0], s_max[:, :, :], -1.0, None, ALU.mult))
            yield from L(v.scalar_tensor_tensor(s_res[:, :, :], s_max[:, :, :], -1.0, max_p[:, :, :, 0], ALU.mult, ALU.subtract))
            yield from L(v.tensor_copy(max_p[:, :, :, 1], s_res[:, :, :]))
            v.tensor_tensor(max_p[:, :, :, 2], s_res[:, :, :], max_p[:, :, :, 1], ALU.subtract).then_inc(S("b_mp"), 1)
            yield
            v.wait_ge(S("b_o9"), b + 1)
            o9 = pd[:, 2, 0:2 * T * VW].rearrange("p (a n) -> p a n", n=VW)
            inv = o_inv[:, :].rearrange("p (a j) -> p a j", j=HG)
            yield from L(v.reciprocal(inv, o9[:, :, HG * DK:VW]))
            v.tensor_tensor(o_n[:, :, :].rearrange("p t (g j d) -> p (t g) j d", g=2, d=DK),
                            o9[:, :, 0:HG * DK].rearrange("p a (j d) -> p a j d", d=DK),
                            inv.unsqueeze(3).broadcast_to([P, 2 * T, HG, DK]), ALU.mult).then_inc(S("b_on"), 1)
            yield
            v.wait_ge(S("b_attn"), b + 1)
            v.wait_ge(S("x3_gone"), 16 * b + 1)
            v.tensor_tensor(x3[:, :, :], x2[:, :, :], pd[:, 1, 0:256].rearrange("p (t n) -> p t n", t=T),
                            ALU.add).then_inc(S("x3_ready"), 1)
            yield
            v.wait_ge(S("x3_ready"), b + 1)
            yield from vector_norm(v, b, 2, x3)
            yield
            lg = pc[:, 256:256 + T * NX].rearrange("p (t e) -> p t e", t=T)
            v.wait_ge(S("b_logits"), b + 1)
            yield from L(v.tensor_reduce(r_max[:, :], lg, AX, ALU.max))
            v.tensor_tensor(r_off[:, :, :], lg, r_max[:, :].unsqueeze(2).broadcast_to([P, T, NX]), ALU.subtract)\
                .then_inc(S("b_roff"), 1)
            yield
            v.wait_ge(S("b_rexp"), b + 1)
            yield from L(v.tensor_reduce(r_sum[:, :], r_exp[:, :, :], AX, ALU.add))
            yield from L(v.reciprocal(r_inv[:, :], r_sum[:, :]))
            v.tensor_tensor(gate_p_all[:, :, bass.ds(b * NX, NX)], r_exp[:, :, :],
                            r_inv[:, :].unsqueeze(2).broadcast_to([P, T, NX]), ALU.mult).then_inc(S("b_gate"), 1)
            assert count_b[0] == DVE_B_STEPS, count_b[0]
            yield

        def part(p, k):
            return p[:, k, :, :].rearrange("p t (h d) -> p (t h) d", d=DK)

        def put(k, first, n, step, p):
            return (stack[:, k, :, first:first + (n - 1) * step + 1:step, :],
                    part(p, k).unsqueeze(2).broadcast_to([P, T * H1N, n, DK]))

        def gpsimd_norm(g, b, n):
            g.wait_ge(S("b_var"), 3 * b + n + 1)
            g.tensor_tensor(rstd_b[:, :], var_b[:, :], neg_half[:, 0:2], ALU.pow).then_inc(S("b_rstd"), 1)

        def gpsimd_b(g, b):
            gpsimd_norm(g, b, 0)
            yield
            gpsimd_norm(g, b, 1)
            yield
            g.wait_ge(S("b_p2"), b + 1)
            for k, where in ((0, 5), (1, 2)):
                g.tensor_tensor(stack[:, k, :, where, :], part(qk_res, k), part(qk_p2, k), ALU.subtract)
            yield
            g.tensor_copy(*put(0, 0, 3, 1, qk_p1))
            yield
            g.tensor_copy(*put(0, 3, 2, 1, qk_p2)).then_inc(S("b_stack"), 1)

            yield
            gpsimd_norm(g, b, 2)
            yield

        SCALE1 = float(DK) ** -0.5

        def scalar_xnt(act, b, n):
            act.wait_ge(S("b_xnt"), 3 * b + n + 1)
            act.activation(xnt_b[:, :], pc[:, 0:256], ACT.Copy).then_inc(S("b_xnts"), 1)

        def scalar_b(act, b):
            scalar_xnt(act, b, 0)
            for c in range(NCH):
                yield
                act.wait_ge(S("b_gu"), 3 * b + c + 1)
                act.activation(tanh_g[:, c, :], pd[:, c, 0:256], ACT.Tanh, scale=0.5).then_inc(S("b_tanh"), 1)
            yield
            scalar_xnt(act, b, 1)
            yield
            act.wait_ge(S("b_qkv"), b + 1)
            act.activation(qk32[:, :, :, :].rearrange("p k t n -> p t k n"),
                           pd[:, 0:2, 0:256].rearrange("p t (k n) -> p t k n", k=2), ACT.Copy).then_inc(S("b_qk32"), 1)
            for t in range(T):
                vv = act.activation(v_own[:, 2 * t:2 * t + 2, :, :], pd[:, t, 256:384].rearrange("p (g j d) -> p g j d", g=2, d=DK),
                                    ACT.Copy)
            vv.then_inc(S("b_v"), 1)
            yield
            act.wait_ge(S("b_qk32"), b + 1)
            flat = lambda a: a[:, :, :, :].rearrange("p k t n -> p (k t n)")
            act.activation(flat(qk_p1), flat(qk32), ACT.Copy).then_inc(S("b_p1"), 1)
            yield
            act.wait_ge(S("b_res"), b + 1)
            act.activation(flat(qk_p2), flat(qk_res), ACT.Copy).then_inc(S("b_p2"), 1)
            yield
            act.activation(*put(1, 0, 2, 3, qk_p1), ACT.Copy)
            yield
            act.activation(*put(1, 5, 1, 1, qk_p1), ACT.Copy)
            yield
            act.wait_ge(S("b_p2"), b + 1)
            act.activation(*put(1, 1, 2, 3, qk_p2), ACT.Copy).then_inc(S("b_stack"), 1)
            for t in range(T):
                yield
                act.wait_ge(S("b_turned"), 4 * b + 2 * t + 1)
                act.activation(stack_t[:, 0, :, t * P:t * P + P], pd_b[:, 2 * t, :].rearrange("p (h n) -> p h n", n=P),
                               ACT.Copy).then_inc(S("b_qt"), 1)
            yield
            act.wait_ge(S("b_mt"), b + 1)
            act.activation(max_t[:, 0:256], pc_b[:, 768:1024], ACT.Copy)
            act.activation(max_t[:, 256:384], pc_b[:, 896:1024], ACT.Copy).then_inc(S("b_mts"), 1)
            for h in range(NPAIR):
                s = h % 2
                yield
                act.wait_ge(S("b_s2"), 8 * b + h + 1)
                if h >= 2:
                    act.wait_ge(S("b_pv"), 8 * b + h - 1)
                act.activation(p_exp[:, s, :, :], pd[:, 2 * s:2 * s + 2, 0:384], ACT.Exp, scale=SCALE1).then_inc(S("b_e"), 1)
            yield
            act.wait_ge(S("b_pv"), 8 * b + 8)
            act.activation(o_raw[0:VW, :], pc[0:VW, :], ACT.Copy).then_inc(S("b_oraw"), 1)
            yield
            act.wait_ge(S("b_ot"), b + 1)
            act.activation(o_t[:, :], pd[:, 0, 0:256], ACT.Copy).then_inc(S("b_ots"), 1)
            yield
            scalar_xnt(act, b, 2)
            yield
            act.wait_ge(S("b_roff"), b + 1)
            act.activation(r_exp[:, :, :], r_off[:, :, :], ACT.Exp).then_inc(S("b_rexp"), 1)
            yield

        def tensor_xnt(pe, b, n):
            pe.wait_ge(S("b_xn"), 6 * b + 2 * n + 2)
            pe.transpose(pc[:, 0:128], xn_b[:, 0, :], ident[:, :])
            pe.transpose(pc[:, 128:256], xn_b[:, 1, :], ident[:, :]).then_inc(S("b_xnt"), 1)
            yield
            pe.wait_ge(S("b_xnts"), 3 * b + n + 1)

        def tensor_b(pe, b):
            yield from tensor_xnt(pe, b, 0)
            for c in range(NCH):
                if c:
                    yield
                pe.matmul(pd[:, c, 0:256], w_gate_t[:, c * P:c * P + P], xnt_b[:, :], start=True, stop=True)
                pe.matmul(pd[:, c, 256:512], w_up_t[:, c * P:c * P + P], xnt_b[:, :], start=True, stop=True)\
                    .then_inc(S("b_gu"), 1)
            yield
            pe.wait_ge(S("b_hid"), 3 * b + 3)
            for t in range(T):
                for c in range(NCH):
                    mm = pe.matmul(pc[:, 256 + t * P:384 + t * P], hid_t[:, c, t * P:t * P + P], w_down_t[:, c, :],
                                   start=(c == 0), stop=(c == NCH - 1))
            mm.then_inc(S("b_ffn"), 1)
            yield
            yield from tensor_xnt(pe, b, 1)
            for t in range(T):
                mm = pe.matmul(pd[:, t, 0:384], xnt_b[:, t * P:t * P + P], w_l1[:, :], start=True, stop=True)
            mm.then_inc(S("b_qkv"), 1)
            yield
            pe.wait_ge(S("b_stack"), 2 * b + 2)
            pe.wait_ge(S("b_v"), b + 1)
            for r in range(4):
                t, k = r // 2, r % 2
                if r:
                    yield
                for h in range(NPAIR):
                    mm = pe.transpose(pd_b[:, r, h * P:h * P + P],
                                      stack[:, k, t * H1N + 2 * h:t * H1N + 2 * h + 2, :, :].rearrange("p g c d -> p (g c d)"),
                                      ident_b[:, :])
                mm.then_inc(S("b_turned"), 1)
            yield
            def qk(k, h, t0, n=1):
                lo = 64 * (h % 2)
                return stack_t[lo:lo + 48, k, h // 2, t0 * P:(t0 + n) * P]

            yield
            pe.wait_ge(S("b_qt"), 2 * b + 2)
            pe.wait_ge(S("b_kt"), 2 * b + 2)
            def on_diagonal(o):
                return o.rearrange("p (a n) -> p a n", n=P)[:, 0:3:2, :]

            for h2 in range(NPAIR):
                yield
                if h2 >= 2:
                    pe.wait_ge(S("b_m1"), 8 * b + h2 - 1)
                for h in (2 * h2, 2 * h2 + 1):
                    o = pd[:, 2 * (h2 % 2) + h % 2, :]
                    pe.matmul(on_diagonal(o), ident_b[:, :], mask_qk[:, :, :], start=True, stop=False, skip_group_check=True)
                    pe.matmul(o[:, 0:128], qk(0, h, 0), qk(1, h, 0), start=False, stop=True, skip_group_check=True)
                    mm = pe.matmul(o[:, 128:384], qk(0, h, 1), qk(1, h, 0, 2), start=False, stop=True, skip_group_check=True)
                mm.then_inc(S("b_s1"), 1)
            yield
            pe.wait_ge(S("b_mp"), b + 1)
            for t in range(T):
                mm = pe.transpose(pc_b[:, 768 + t * P:896 + t * P], max_pad[:, t, :], ident_b[:, :])
            mm.then_inc(S("b_mt"), 1)

            def scores(h2):
                if h2 >= 2:
                    pe.wait_ge(S("b_e"), 8 * b + h2 - 1)
                for h in (2 * h2, 2 * h2 + 1):
                    o = pd[:, 2 * (h2 % 2) + h % 2, :]
                    pe.matmul(on_diagonal(o), ident_b[:, :], mask_kq[:, :, :], start=True, stop=False, skip_group_check=True)
                    pe.matmul(o[:, 0:384], pick_head[:, h, :], max_t[:, :], start=False, stop=False, skip_group_check=True)
                    pe.matmul(o[:, 0:256], qk(1, h, 0), qk(0, h, 0, 2), start=False, stop=True, skip_group_check=True)
                    mm = pe.matmul(o[:, 256:384], qk(1, h, 1), qk(0, h, 1), start=False, stop=True, skip_group_check=True)
                mm.then_inc(S("b_s2"), 1)

            def values(h2):
                pe.wait_ge(S("b_e"), 8 * b + h2 + 1)
                for h in (2 * h2, 2 * h2 + 1):
                    p = p_exp[:, h2 % 2, h % 2, :]
                    g, j = divmod(h, HG)
                    v_of = lambda t: v_pad[:, 2 * t + g, j * VW:j * VW + VW]
                    o = pc[0:VW, g * 256:g * 256 + 256]
                    pe.matmul(o, v_of(0), p[:, 0:256], start=(j == 0), stop=False, skip_group_check=True)
                    mm = pe.matmul(o[:, 128:256], v_of(1), p[:, 256:384], start=False, stop=(j == HG - 1), skip_group_check=True)
                mm.then_inc(S("b_pv"), 1)

            for h2 in range(NPAIR + 1):
                if h2 < NPAIR:
                    yield
                    if h2 == 0:
                        pe.wait_ge(S("b_mts"), b + 1)
                    scores(h2)
                if h2 >= 1:
                    yield
                    values(h2 - 1)
            yield
            pe.wait_ge(S("b_oraw"), b + 1)
            for t in range(T):
                for g in range(2):
                    mm = pe.transpose(pd[:, 2, (2 * t + g) * VW:(2 * t + g) * VW + VW],
                                      o_raw[0:VW, g * 256 + t * P:g * 256 + t * P + P], ident[0:VW, 0:VW])
            mm.then_inc(S("b_o9"), 1)
            yield
            pe.wait_ge(S("b_on"), b + 1)
            pe.transpose(pd[:, 0, 0:128], o_n[:, 0, :], ident[:, :])
            pe.transpose(pd[:, 0, 128:256], o_n[:, 1, :], ident[:, :]).then_inc(S("b_ot"), 1)
            yield
            pe.wait_ge(S("b_ots"), b + 1)
            for t in range(T):
                mm = pe.matmul(pd[:, 1, t * P:t * P + P], o_t[:, t * P:t * P + P], w_o[:, :], start=True, stop=True)
            mm.then_inc(S("b_attn"), 1)
            yield
            yield from tensor_xnt(pe, b, 2)
            for t in range(T):
                mm = pe.matmul(pc[:, 256 + t * NX:256 + t * NX + NX], xnt_b[:, t * P:t * P + P], w_route_t[:, :],
                               start=True, stop=True)
            mm.then_inc(S("b_logits"), 1)
            yield

        tiles = lambda a: a.rearrange("(t p) e -> p t e", p=P)

        def sync_a(sp, b):
            sp.wait_ge(S("x_taken"), b)
            sp.dma_start(x_land[:, :, :], tiles(x_in[b])).then_inc(S("x_in"), 16)

        def sync_b(sp, b):
            sp.wait_ge(S("x3_ready"), b + 1)
            sp.dma_start(tiles(x3_d[b]), x3[:, :, :]).then_inc(S("x3_gone"), 16)
            sp.wait_ge(S("b_xn"), 6 * b + 6)
            sp.dma_start(tiles(xn4_d[b]), xn_b[:, :, :]).then_inc(S("xn4_gone"), 16)

        def vector_choose(v):
            n = [0]

            def link(ins):
                n[0] += 1
                ins.then_inc(S("dve_choose"), 1)
                v.wait_ge(S("dve_choose"), n[0])

            v.wait_ge(S("rows_turned"), 1)
            R = ROWS
            for h in range(HALVES):
                link(v.tensor_copy(g_rows[0:R, h, :], pd[0:R, h, 0:256]))
            link(v.memset(g_one, 1.0))
            src = g_rows
            for k in range(CAP // 8):
                for h in range(HALVES):
                    v.max(g_top[0:R, h, :], src[0:R, h, :]).then_inc(S("dve_choose"), 1)
                    n[0] += 1
                v.wait_ge(S("dve_choose"), n[0])
                for h in range(HALVES):
                    v.match_replace(g_left[0:R, h, :], g_top[0:R, h, :], src[0:R, h, :], -1.0).then_inc(S("dve_choose"), 1)
                    n[0] += 1
                v.wait_ge(S("dve_choose"), n[0])
                src = g_left
            for h in range(HALVES):
                link(v.tensor_scalar(g_mask[0:R, h, :], g_left[0:R, h, :], 0.0, None, ALU.is_lt))
                link(v.tensor_tensor_scan(g_rank[0:R, h, :], g_one[0:R, :], g_mask[0:R, h, :], 0.0, ALU.mult, ALU.add))
                link(v.tensor_tensor(g_rank[0:R, h, :], g_rank[0:R, h, :], g_mask[0:R, h, :], ALU.mult))
                link(v.tensor_scalar(g_rank[0:R, h, :], g_rank[0:R, h, :], -1.0, None, ALU.add))
            v.tensor_copy(g_top[0:R, 0, 0:1], g_one[0:R, 0:1]).then_inc(S("ranks"), 1)
            v.wait_ge(S("slots_turned"), 1)
            for t in range(T):
                for h in range(HALVES):
                    link(v.tensor_copy(slots[:, t, h * R:h * R + R], pd[:, 2 + t, h * 128:h * 128 + R]))
            v.tensor_copy(spare[:, 3:4], g_one[:, 0:1]).then_inc(S("chosen"), 1)
            v.wait_ge(S("chosen"), 1)

        def tensor_choose(pe):
            pe.wait_ge(S("b_gate"), B)
            R = ROWS
            for h in range(HALVES):
                for t in range(T):
                    mm = pe.transpose(pd[0:R, h, t * P:t * P + P], gate_p_all[:, t, h * R:h * R + R], ident[:, :])
            mm.then_inc(S("rows_turned"), 1)
            pe.wait_ge(S("ranks"), 1)
            for t in range(T):
                for h in range(HALVES):
                    mm = pe.transpose(pd[:, 2 + t, h * 128:h * 128 + R], g_rank[0:R, h, t * P:t * P + P], ident[0:R, 0:R])
            mm.then_inc(S("slots_turned"), 1)

        NM = GRP // 2
        PAIRS_FREE = {"c_sel": 3, "c_turned": 5, "c_added": 2, "out_gone_0": 1, "out_gone_1": 1}


        def load_xn(sp, g, m):
            sp.wait_ge(S("c_sel"), 2 * (g * NM + m) + 1)
            sp.dma_start(xn_pair[m % 2].rearrange("p b t e -> p (b t) e"), pairs(xn4_d, g, m)).then_inc(S(f"c_xn_in_{m % 2}"), 16)

        def load_x3(sp, g, m):
            sp.wait_ge(S("c_added"), g * NM + m + 1)
            sp.dma_start(x3_pair[m % 2].rearrange("p b t e -> p (b t) e"), pairs(x3_d, g, m)).then_inc(S(f"c_x3_in_{m % 2}"), 16)

        def store_out(sp, g, m):
            sp.wait_ge(S("c_added"), g * NM + m + 3)
            sp.dma_start(pairs(out, g, m), y_out[m % 2].rearrange("p b t e -> p (b t) e")).then_inc(S(f"out_gone_{m % 2}"), 16)

        def sync_experts(sp, g, last):
            for m in range(2, NM):
                load_xn(sp, g, m)
            load_x3(sp, g, 0)
            load_x3(sp, g, 1)
            if not last:
                load_xn(sp, g + 1, 0)
                load_xn(sp, g + 1, 1)
            for m in range(NM):
                store_out(sp, g, m)
                if m + 2 < NM:
                    load_x3(sp, g, m + 2)

        def pairs(d, g, m):
            flat = d.rearrange("b (t p) e -> p (b t) e", p=P)
            return flat[:, bass.ds(g * (GRP * T) + m * 2 * T, 2 * T), :]

        def oh(a, b):
            return a[:, b, :, :].rearrange("p t (e s) -> p t e s", s=CAP)

        def gate_columns(g, m, b):
            return bass.ds(g * (GRP * NX) + (2 * m + b) * NX, NX)

        def vector_experts(v, g):
            def make_onehot(m):
                v.wait_ge(S("c_sel"), 2 * NM * g + 2 * m + 1)
                for b in range(2):
                    where = slots[:, :, gate_columns(g, m, b)].unsqueeze(3).broadcast_to([P, T, NX, CAP])
                    v.tensor_tensor(oh(onehot[m % 2], b), slot_ids[:, :].unsqueeze(1).unsqueeze(1).broadcast_to([P, T, NX, CAP]),
                                    where, ALU.is_equal).then_inc(S("c_onehot"), 1)

            def keep_spread(m):
                for k in range(4):
                    v.wait_ge(S("c_turned"), 4 * NM * g + 4 * m + k + 6)
                    v.tensor_copy(spread_flat[:, m * 2048 + k * 512:m * 2048 + k * 512 + 512], pd[:, k, :]).then_inc(S("c_spread"), 1)

            make_onehot(0)
            for m in range(NM):
                if m + 1 < NM:
                    make_onehot(m + 1)
                keep_spread(m)
            for e in range(NX):
                v.wait_ge(S("c_y"), NX * g + e + 1)
                v.tensor_copy(y_exp[:, e, :, :].rearrange("p m n -> p (m n)"), pa[:, e % 2, :]).then_inc(S("c_yexp"), 1)
            for m in range(NM):
                v.wait_ge(S(f"c_x3_in_{m % 2}"), 16 * (NM // 2 * g + m // 2) + 16)
                v.wait_ge(S("c_scattered"), NM * g + m + 1)
                v.wait_ge(S(f"out_gone_{m % 2}"), 16 * (NM // 2 * g + m // 2) + 1)
                for b, bank in enumerate(banks(m)):
                    y = v.tensor_tensor(y_out[m % 2][:, b, :, :].rearrange("p t e -> p (t e)"),
                                        x3_pair[m % 2][:, b, :, :].rearrange("p t e -> p (t e)"), bank[:, 0:256], ALU.add)
                y.then_inc(S("c_added"), 1)

        def banks(m):
            return (pc, pb) if m % 2 == 0 else (pd[:, 0, :], pd[:, 1, :])

        def gpsimd_experts(gp, g):
            for m in range(NM):
                gp.wait_ge(S("c_turned"), 4 * NM * g + 4 * m + 1)
                for b in range(2):
                    weight = gate_p_all[:, :, gate_columns(g, m, b)].unsqueeze(3).broadcast_to([P, T, NX, CAP])
                    gp.wait_ge(S("c_onehot"), 2 * NM * g + 2 * m + b + 1)
                    gp.tensor_tensor(weighted[m % 2][:, :, :, b * CAP:b * CAP + CAP], oh(onehot[m % 2], b), weight,
                                     ALU.mult).then_inc(S("c_weighted"), 1)

        def scalar_experts(act, g):
            for m in range(NM):
                for b in range(2):
                    act.wait_ge(S("c_sel"), GRP * g + 2 * m + b + 4)
                    act.activation(x_sel[:, :, 2 * m + b, :], pa[:, b, :].rearrange("p (e s) -> p e s", s=CAP),
                                   ACT.Copy).then_inc(S("c_xsel"), 1)
            for e in range(NX):
                for f in range(NF):
                    act.wait_ge(S("c_h"), NX * NF * g + NF * e + f + 1)
                    if f == 0 and e >= 2:
                        act.wait_ge(S("c_y"), NX * g + e - 1)
                    act.activation(h_act[:, e % 2, f, :], pd[:, f, :], ACT.Gelu_apprx_tanh, bias=b1[:, e, f:f + 1])\
                        .then_inc(S("c_gelu"), 1)

        def tensor_experts(pe, g):
            for m in range(NM):
                pe.wait_ge(S(f"c_xn_in_{m % 2}"), 16 * (NM // 2 * g + m // 2) + 16)
                pe.wait_ge(S("c_onehot"), 2 * NM * g + 2 * m + 2)
                for b in range(2):
                    if m:
                        pe.wait_ge(S("c_xsel"), GRP * g + 2 * m + b - 1)
                    for t in range(T):
                        mm = pe.matmul(pa[:, b, :], xn_pair[m % 2][:, b, t, :], onehot[m % 2][:, b, t, :],
                                       start=(t == 0), stop=(t == T - 1))
                    mm.then_inc(S("c_sel"), 1)
                pe.wait_ge(S("c_weighted"), 2 * NM * g + 2 * m + 2)
                if m:
                    pe.wait_ge(S("c_spread"), 4 * NM * g + 4 * m)
                else:
                    pe.wait_ge(S("c_added"), NM * g + 2)
                for k in range(4):
                    for j in range(4):
                        t, e = divmod(4 * k + j, NX)
                        mm = pe.transpose(pd[:, k, j * P:j * P + P], weighted[m % 2][:, t, e, :], ident[:, :])
                    mm.then_inc(S("c_turned"), 1)
            pe.wait_ge(S("c_xsel"), GRP * g + GRP)
            pe.wait_ge(S("c_spread"), 4 * NM * g + 4 * NM)

            def up(e):
                for f in range(NF):
                    if e:
                        pe.wait_ge(S("c_gelu"), NX * NF * g + NF * (e - 1) + f + 1)
                    pe.matmul(pd[:, f, :], w1[:, e, f * P:f * P + P], x_sel[:, e, :, :].rearrange("p b s -> p (b s)"),
                              start=True, stop=True).then_inc(S("c_h"), 1)

            def down(e):
                pe.wait_ge(S("c_gelu"), NX * NF * g + NF * e + NF)
                if e >= 2:
                    pe.wait_ge(S("c_yexp"), NX * g + e - 1)
                for m in range(NM):
                    o = pa[:, e % 2, m * E:m * E + E]
                    pe.matmul(o, ones_row[:, :], b2_row[:, e, :], start=True, stop=False)
                    for f in range(NF):
                        mm = pe.matmul(o, h_act[:, e % 2, f, m * P:m * P + P], w2[:, e, f, :], start=False, stop=(f == NF - 1))
                mm.then_inc(S("c_y"), 1)

            for e in range(NX + 1):
                if e < NX:
                    up(e)
                if e:
                    down(e - 1)
            pe.wait_ge(S("c_yexp"), NX * g + NX)
            for m in range(NM):
                pe.wait_ge(S("c_added"), NM * g + m + 1)
                for t in range(T):
                    for e in range(NX):
                        for b, bank in enumerate(banks(m)):
                            lo = b * CAP
                            mm = pe.matmul(bank[:, t * E:t * E + E], spread[lo:lo + CAP, m, t, e, :],
                                           y_exp[lo:lo + CAP, e, m, :], start=(e == 0), stop=(e == NX - 1))
                mm.then_inc(S("c_scattered"), 1)

        def pieces_of(order):
            runs = order.replace("A", " A").replace("B", " B").split()
            return "".join(r[0] * int(r[1:]) for r in runs)

        def both(stage_a, stage_b, eng, b, order):
            run = {"A": stage_a(eng, b), "B": stage_b(eng, b - 1)}
            for s in pieces_of(order):
                next(run[s])
            assert all(next(r, None) is None for r in run.values())

        def alone(stage, eng, b):
            for _ in stage(eng, b):
                pass

        def sequences(stage_a, stage_b, eng, order):
            alone(stage_a, eng, 0)
            with eng.Fori(1, B) as b:
                both(stage_a, stage_b, eng, b, order)
            alone(stage_b, eng, B - 1)

        block = ctx.enter_context(nc.Block())

        @block.sync
        def _(sp):
            setup_sync(sp)
            sp.dma_start(x_land[:, :, :], tiles(x_in[0])).then_inc(S("x_in"), 16)
            with sp.Fori(1, B) as b:
                sync_a(sp, b)
                sync_b(sp, b - 1)
            sync_b(sp, B - 1)
            sp.wait_ge(S("x3_gone"), 16 * B + 1)
            sp.wait_ge(S("xn4_gone"), 16 * B + 1)
            sp.wait_ge(S("chosen"), 1)
            load_xn(sp, 0, 0)
            load_xn(sp, 0, 1)
            if NG > 1:
                with sp.Fori(0, NG - 1) as g:
                    sync_experts(sp, g, False)
            sync_experts(sp, NG - 1, True)
            for i in range(2):
                sp.wait_ge(S(f"out_gone_{i}"), 16 * (NM // 2) * NG + 1)

        @block.gpsimd
        def _(g):
            setup_gpsimd(g)
            sequences(gpsimd_a, gpsimd_b, g, POOL_ORDER)
            g.wait_ge(S("chosen"), 1)
            with g.Fori(0, NG) as group:
                gpsimd_experts(g, group)

        @block.scalar
        def _(act):
            setup_scalar_dma(act)
            setup_scalar(act)
            act.wait_ge(S("pool_setup"), POOL_SETUP)
            sequences(scalar_a, scalar_b, act, ACT_ORDER)
            act.wait_ge(S("experts_in"), EXPERTS_IN)
            with act.Fori(0, NG) as g:
                scalar_experts(act, g)

        @block.tensor
        def _(pe):
            setup_tensor(pe)
            sequences(tensor_a, tensor_b, pe, PE_ORDER)
            tensor_choose(pe)
            pe.wait_ge(S("experts_in"), EXPERTS_IN)
            with pe.Fori(0, NG) as g:
                tensor_experts(pe, g)

        @block.vector
        def _(v):
            setup_vector(v)
            for name in ("x3_gone", "xn4_gone"):
                v.sem_inc(S(name), 1)
            for name, count in PAIRS_FREE.items():
                v.sem_inc(S(name), count)
            v.wait_ge(S("pool_setup"), POOL_SETUP)
            sequences(vector_a, vector_b, v, DVE_ORDER)
            vector_choose(v)
            with v.Fori(0, NG) as g:
                vector_experts(v, g)


_INS = ["L0_attn_query", "L0_attn_W_qkv", "L0_attn_b_qkv", "L0_attn_W_out", "L0_attn_b_out",
        "L0_attn_quantum_weights", "L0_attn_photonic_phases", "L0_attn_entanglement_gates",
        "L0_attn_superposition_logits", "L0_ffn_w_gate", "L0_ffn_w_up", "L0_ffn_w_down",
        "L1_attn_Wq", "L1_attn_Wk", "L1_attn_Wv", "L1_attn_Wo",
        "L1_ffn_Wg", "L1_ffn_W1", "L1_ffn_b1", "L1_ffn_W2", "L1_ffn_b2"]


def kernel(**inputs):
    import numpy as _np
    import concourse.bacc as _bacc
    from concourse import mybir as _mybir
    from concourse.bass_utils import run_bass_kernel_spmd as _run

    nc = _bacc.Bacc("TRN2", target_bir_lowering=False, num_devices=1)
    arrays, args = {}, {}
    for name in _INS:
        a = _np.ascontiguousarray(inputs[name])
        arrays[f"in_{name}"] = a
        args[name] = nc.dram_tensor(f"in_{name}", a.shape, _mybir.dt.from_np(a.dtype), kind="ExternalInput").ap()
    shape = inputs["L0_attn_query"].shape
    out = nc.dram_tensor("out_x", shape, _mybir.dt.float32, kind="ExternalOutput").ap()
    build(nc, args, out)
    r = _run(nc, [arrays], core_ids=[0])
    return r.results[0]["out_x"]
```
